# Optimizing a Trainium2 kernel written in Bass

```python
import numpy as np
import jax
import jax.numpy as jnp

def _softmax(x, axis=-1):
    return jax.nn.softmax(x, axis=axis)

def _gelu(x):
    return jax.nn.gelu(x, approximate=True)

def _silu(x):
    return jax.nn.silu(x)

def _sigmoid(x):
    return jax.nn.sigmoid(x)

def _layernorm(x, axis=-1, eps=1e-05):
    m = jnp.mean(x, axis=axis, keepdims=True)
    v = jnp.var(x, axis=axis, keepdims=True)
    return (x - m) / jnp.sqrt(v + eps)

def _scatter_add(tgt, idx, src, axis=0):
    return tgt.at[idx].add(src)

def _segment_sum(src, seg, n):
    return jax.ops.segment_sum(src, seg, n)
kernel_name = 'mk_recurrent_d4_jaxref_r8_752bb3'

def setup_inputs(seed: int=0):
    np.random.seed(seed)
    _w = jnp.asarray

    def _L0_attn_setup():
        import jax, jax.numpy as jnp
        import numpy as np
        EMBED_DIM = 128
        NUM_HEADS = 16
        CONTEXT = 250
        MAX_PERIOD = 10000.0
        HEAD_DIM = EMBED_DIM // NUM_HEADS

        def _apply_rope(q, k):
            B, H, T, D = q.shape
            ds = jnp.arange(D // 2, dtype=jnp.float32)
            freqs = jnp.exp(ds * (-np.log(MAX_PERIOD) * 2.0 / D))
            ts = jnp.arange(T, dtype=jnp.float32)
            ang = ts[:, None] * freqs[None, :]
            cos = jnp.cos(ang)
            sin = jnp.sin(ang)

            def rot(x):
                xr = x.reshape(B, H, T, D // 2, 2)
                xa, xb = (xr[..., 0], xr[..., 1])
                ya = xa * cos - xb * sin
                yb = xa * sin + xb * cos
                return jnp.stack([ya, yb], axis=-1).reshape(B, H, T, D)
            return (rot(q), rot(k))
        key = jax.random.key(seed)
        k1, k2, k3 = jax.random.split(key, 3)
        B, T = (2, 256)
        query = jax.random.normal(k1, (B, T, EMBED_DIM), jnp.float32)
        in_proj_w = jax.random.normal(k2, (3 * EMBED_DIM, EMBED_DIM), jnp.float32) * EMBED_DIM ** (-0.5)
        out_proj_w = jax.random.normal(k3, (EMBED_DIM, EMBED_DIM), jnp.float32) * EMBED_DIM ** (-0.5)
        return {'query': query, 'in_proj_w': in_proj_w, 'out_proj_w': out_proj_w}
    _L0_attn_in = _L0_attn_setup()

    def _L0_ffn_setup():
        import jax, jax.numpy as jnp
        import numpy as np
        DIM = 128

        def _reference_tuple_inner(x, W_r, W_k, W_v, mu_r, mu_k):
            B, T, C = x.shape
            x_prev = jnp.concatenate([jnp.zeros((B, 1, C), x.dtype), x[:, :-1, :]], axis=1)
            xr = mu_r * x + (1.0 - mu_r) * x_prev
            xk = mu_k * x + (1.0 - mu_k) * x_prev
            r = jax.nn.sigmoid(jnp.einsum('btc,dc->btd', xr, W_r))
            k = jnp.einsum('btc,dc->btd', xk, W_k)
            k_act = jnp.square(jax.nn.relu(k))
            out = r * jnp.einsum('btc,dc->btd', k_act, W_v)
            new_state = x[:, -1, :]
            return (out, new_state)
        key = jax.random.key(seed)
        ks = jax.random.split(key, 6)
        B, T, C = (8, 256, DIM)
        x = jax.random.normal(ks[0], (B, T, C), dtype=jnp.float32)
        s = 1.0 / np.sqrt(C)
        W_r = jax.random.uniform(ks[1], (C, C), jnp.float32, -s, s)
        W_k = jax.random.uniform(ks[2], (C, C), jnp.float32, -s, s)
        W_v = jax.random.uniform(ks[3], (C, C), jnp.float32, -s, s)
        mu_r = jax.random.uniform(ks[4], (C,), jnp.float32)
        mu_k = jax.random.uniform(ks[5], (C,), jnp.float32)
        return {'x': x, 'W_r': W_r, 'W_k': W_k, 'W_v': W_v, 'mu_r': mu_r, 'mu_k': mu_k}
    _L0_ffn_in = _L0_ffn_setup()

    def _L1_attn_setup():
        import jax, jax.numpy as jnp
        import numpy as np
        D_MODEL = 128
        N_HEADS = 16
        D_HEAD = D_MODEL // N_HEADS
        key = jax.random.key(seed)
        ks = jax.random.split(key, 9)
        B, S = (2, 256)
        s = 0.02
        return {'x': jax.random.normal(ks[0], (B, S, D_MODEL), dtype=jnp.float32), 'Wq': jax.random.normal(ks[1], (D_MODEL, D_MODEL), dtype=jnp.float32) * s, 'bq': jnp.zeros((D_MODEL,), dtype=jnp.float32), 'Wk': jax.random.normal(ks[2], (D_MODEL, D_MODEL), dtype=jnp.float32) * s, 'bk': jnp.zeros((D_MODEL,), dtype=jnp.float32), 'Wv': jax.random.normal(ks[3], (D_MODEL, D_MODEL), dtype=jnp.float32) * s, 'bv': jnp.zeros((D_MODEL,), dtype=jnp.float32), 'Wo': jax.random.normal(ks[4], (D_MODEL, D_MODEL), dtype=jnp.float32) * s, 'bo': jnp.zeros((D_MODEL,), dtype=jnp.float32)}
    _L1_attn_in = _L1_attn_setup()

    def _L1_ffn_setup():
        import jax, jax.numpy as jnp
        import numpy as np
        B, S, D, H, E, K = (4, 256, 128, 256, 8, 2)
        TEMP = 5.0
        EPS = 1e-09
        key = jax.random.key(seed)
        k_x, k_wg, k_w1, k_w2 = jax.random.split(key, 4)
        scale = 0.02
        return {'x': jax.random.normal(k_x, (B, S, D), dtype=jnp.float32), 'Wg': jax.random.normal(k_wg, (D, E), dtype=jnp.float32) * scale, 'bg': jnp.zeros((E,), dtype=jnp.float32), 'W1': jax.random.normal(k_w1, (E, D, H), dtype=jnp.float32) * scale, 'b1': jnp.zeros((E, H), dtype=jnp.float32), 'W2': jax.random.normal(k_w2, (E, H, D), dtype=jnp.float32) * scale, 'b2': jnp.zeros((E, D), dtype=jnp.float32)}
    _L1_ffn_in = _L1_ffn_setup()

    def _L2_attn_setup():
        import jax, jax.numpy as jnp
        import numpy as np
        D_MODEL = 128
        NUM_HEADS = 16
        HEAD_DIM = D_MODEL // NUM_HEADS
        D_FF = 512
        EPS = 1e-05

        def layer_norm(x, gamma, beta):
            mu = jnp.mean(x, axis=-1, keepdims=True)
            var = jnp.mean((x - mu) ** 2, axis=-1, keepdims=True)
            return (x - mu) * jax.lax.rsqrt(var + EPS) * gamma + beta

        def apply_rope(t):
            S, d = (t.shape[-2], t.shape[-1])
            inv_freq = 1.0 / 10000.0 ** (jnp.arange(0, d, 2, dtype=jnp.float32) / d)
            angles = jnp.arange(S, dtype=jnp.float32)[:, None] * inv_freq[None, :]
            sin, cos = (jnp.sin(angles), jnp.cos(angles))
            tp = t.reshape(*t.shape[:-1], d // 2, 2)
            t0, t1 = (tp[..., 0], tp[..., 1])
            rot = jnp.stack([t0 * cos - t1 * sin, t0 * sin + t1 * cos], axis=-1)
            return rot.reshape(t.shape)
        key = jax.random.key(seed)
        ks = jax.random.split(key, 18)
        s = 0.02
        d, f = (D_MODEL, D_FF)
        return {'x': jax.random.normal(ks[0], (2, 256, d), dtype=jnp.float32), 'Wq': jax.random.normal(ks[1], (d, d), dtype=jnp.float32) * s, 'bq': jnp.zeros((d,), jnp.float32), 'Wk': jax.random.normal(ks[2], (d, d), dtype=jnp.float32) * s, 'bk': jnp.zeros((d,), jnp.float32), 'Wv': jax.random.normal(ks[3], (d, d), dtype=jnp.float32) * s, 'bv': jnp.zeros((d,), jnp.float32), 'Wo': jax.random.normal(ks[4], (d, d), dtype=jnp.float32) * s, 'bo': jnp.zeros((d,), jnp.float32), 'W1': jax.random.normal(ks[5], (d, f), dtype=jnp.float32) * s, 'b1': jnp.zeros((f,), jnp.float32), 'W2': jax.random.normal(ks[6], (f, d), dtype=jnp.float32) * s, 'b2': jnp.zeros((d,), jnp.float32), 'g1': jnp.ones((d,), jnp.float32), 'beta1': jnp.zeros((d,), jnp.float32), 'g2': jnp.ones((d,), jnp.float32), 'beta2': jnp.zeros((d,), jnp.float32)}
    _L2_attn_in = _L2_attn_setup()

    def _L2_ffn_setup():
        import jax, jax.numpy as jnp
        import numpy as np
        NUM_EXPERTS = 8
        CAPACITY = 80
        key = jax.random.key(seed)
        ks = jax.random.split(key, 5)
        D, E, F = (128, NUM_EXPERTS, 512)
        inputs = jax.random.normal(ks[0], (2, 256, D), dtype=jnp.float32)
        gate_w = jax.random.normal(ks[1], (D, E), dtype=jnp.float32) * 0.02
        gate_b = jnp.zeros((E,), dtype=jnp.float32)
        w1 = jax.random.normal(ks[2], (E, D, F), dtype=jnp.float32) * 0.02
        b1 = jnp.zeros((E, F), dtype=jnp.float32)
        w2 = jax.random.normal(ks[3], (E, F, D), dtype=jnp.float32) * 0.02
        b2 = jnp.zeros((E, D), dtype=jnp.float32)
        return {'inputs': inputs, 'gate_w': gate_w, 'gate_b': gate_b, 'w1': w1, 'b1': b1, 'w2': w2, 'b2': b2}
    _L2_ffn_in = _L2_ffn_setup()

    def _L3_attn_setup():
        import jax, jax.numpy as jnp
        import numpy as np
        from jax import lax
        C = 128
        D_STATE = 64
        D_CONV = 4
        EXPAND = 2
        HEADDIM = 64
        D_INNER = EXPAND * C
        NHEADS = D_INNER // HEADDIM
        NGROUPS = 1
        D_CONVDIM = D_INNER + 2 * NGROUPS * D_STATE
        D_INPROJ = 2 * D_INNER + 2 * NGROUPS * D_STATE + NHEADS
        EPS = 1e-05

        def _mamba_block(h, ln_w, ln_b, in_proj_w, conv_w, conv_b, dt_bias, A_log, Dvec, rms_w, out_proj_w):
            N, T, _ = h.shape
            res = h
            mu = jnp.mean(h, -1, keepdims=True)
            var = jnp.mean(jnp.square(h - mu), -1, keepdims=True)
            hn = (h - mu) * lax.rsqrt(var + EPS) * ln_w + ln_b
            zxbcdt = jnp.einsum('btc,dc->btd', hn, in_proj_w)
            z = zxbcdt[..., :D_INNER]
            xBC = zxbcdt[..., D_INNER:D_INNER + D_CONVDIM]
            dt = jax.nn.softplus(zxbcdt[..., D_INNER + D_CONVDIM:] + dt_bias)
            xp = jnp.pad(xBC, ((0, 0), (D_CONV - 1, 0), (0, 0)))
            conv = conv_b
            for k in range(D_CONV):
                conv = conv + xp[:, k:k + T, :] * conv_w[:, k]
            xBC = jax.nn.silu(conv)
            x = xBC[..., :D_INNER].reshape(N, T, NHEADS, HEADDIM)
            B = xBC[..., D_INNER:D_INNER + D_STATE]
            Cc = xBC[..., D_INNER + D_STATE:]
            A = -jnp.exp(A_log)
            dA = jnp.exp(dt * A)

            def step(state, inp):
                dA_t, dt_t, x_t, B_t, C_t = inp
                state = state * dA_t[:, :, None, None] + (dt_t[:, :, None] * x_t)[..., None] * B_t[:, None, None, :]
                y = jnp.einsum('bhpn,bn->bhp', state, C_t)
                return (state, y)
            xs = (jnp.moveaxis(dA, 1, 0), jnp.moveaxis(dt, 1, 0), jnp.moveaxis(x, 1, 0), jnp.moveaxis(B, 1, 0), jnp.moveaxis(Cc, 1, 0))
            state0 = jnp.zeros((N, NHEADS, HEADDIM, D_STATE), x.dtype)
            _, ys = lax.scan(step, state0, xs)
            y = jnp.moveaxis(ys, 0, 1) + Dvec[None, None, :, None] * x
            y = y.reshape(N, T, D_INNER)
            y = y * jax.nn.silu(z)
            y = y * lax.rsqrt(jnp.mean(jnp.square(y), -1, keepdims=True) + EPS) * rms_w
            out = jnp.einsum('btd,cd->btc', y, out_proj_w)
            return res + out
        key = jax.random.key(seed)
        ks = jax.random.split(key, 8)
        N, T = (4, 256)
        h = jax.random.normal(ks[0], (N, T, C), jnp.float32)
        ln_w = jnp.ones((C,), jnp.float32)
        ln_b = jnp.zeros((C,), jnp.float32)
        in_proj_w = jax.random.normal(ks[1], (D_INPROJ, C), jnp.float32) / np.float32(np.sqrt(C))
        conv_w = jax.random.normal(ks[2], (D_CONVDIM, D_CONV), jnp.float32) * 0.3
        conv_b = jnp.zeros((D_CONVDIM,), jnp.float32)
        dt = jax.random.uniform(ks[3], (NHEADS,), jnp.float32, 0.001, 0.1)
        dt_bias = dt + jnp.log(-jnp.expm1(-dt))
        A_log = jnp.log(jax.random.uniform(ks[4], (NHEADS,), jnp.float32, 1.0, 8.0))
        Dvec = jnp.ones((NHEADS,), jnp.float32)
        rms_w = jnp.ones((D_INNER,), jnp.float32)
        out_proj_w = jax.random.normal(ks[5], (C, D_INNER), jnp.float32) / np.float32(np.sqrt(D_INNER))
        return {'h': h, 'ln_w': ln_w, 'ln_b': ln_b, 'in_proj_w': in_proj_w, 'conv_w': conv_w, 'conv_b': conv_b, 'dt_bias': dt_bias, 'A_log': A_log, 'Dvec': Dvec, 'rms_w': rms_w, 'out_proj_w': out_proj_w}
    _L3_attn_in = _L3_attn_setup()

    def _L3_ffn_setup():
        import jax, jax.numpy as jnp
        import numpy as np
        DIM = 128
        DEPTH = 2
        HEADS = 8
        DIM_HEAD = 64
        WINDOW = 64
        INNER = HEADS * DIM_HEAD
        HID = int(DIM * 4 * 2 / 3)
        B, N = (2, 1024)
        QK_SCALE = 8.0

        def shift_token(t):
            t1, t2 = jnp.split(t, 2, axis=-1)
            t2 = jnp.pad(t2, ((0, 0), (1, 0), (0, 0)))[:, :-1]
            return jnp.concatenate([t1, t2], axis=-1)

        def l2norm(t):
            return t / jnp.clip(jnp.linalg.norm(t, axis=-1, keepdims=True), 1e-12)

        def rotate_half(x):
            x1, x2 = jnp.split(x, 2, axis=-1)
            return jnp.concatenate([-x2, x1], axis=-1)

        def rotary_xpos(q, k):
            n = q.shape[-2]
            half_idx = jnp.arange(0, DIM_HEAD, 2, dtype=jnp.float32)
            inv_freq = 1.0 / 10000.0 ** (half_idx / DIM_HEAD)
            t = jnp.arange(n, dtype=jnp.float32)
            freqs = t[:, None] * inv_freq[None, :]
            freqs = jnp.concatenate([freqs, freqs], axis=-1)
            base = (half_idx + 0.4 * DIM_HEAD) / (1.4 * DIM_HEAD)
            power = (t - n // 2) / float(WINDOW // 2)
            scale = base[None, :] ** power[:, None]
            scale = jnp.concatenate([scale, scale], axis=-1)
            cos, sin = (jnp.cos(freqs), jnp.sin(freqs))
            q = q * cos * scale + rotate_half(q) * sin * scale
            k = k * cos / scale + rotate_half(k) * sin / scale
            return (q, k)

        def local_attention(q, k, v):
            b, h, n, d = q.shape
            w = n // WINDOW
            bq = q.reshape(b, h, w, WINDOW, d) * QK_SCALE
            bk = k.reshape(b, h, w, WINDOW, d)
            bv = v.reshape(b, h, w, WINDOW, d)

            def look_around(t):
                p = jnp.pad(t, ((0, 0), (0, 0), (1, 0), (0, 0), (0, 0)))
                return jnp.concatenate([p[:, :, :w], p[:, :, 1:]], axis=3)
            bk, bv = (look_around(bk), look_around(bv))
            bt = jnp.arange(n).reshape(w, WINDOW)
            btp = jnp.pad(bt, ((1, 0), (0, 0)), constant_values=-1)
            btk = jnp.concatenate([btp[:w], btp[1:]], axis=1)
            sim = jnp.einsum('bhwid,bhwjd->bhwij', bq, bk)
            i = bt[:, :, None]
            j = btk[:, None, :]
            mask = (i < j) | (i > j + WINDOW) | (j == -1)
            sim = jnp.where(mask, -jnp.finfo(sim.dtype).max, sim)
            attn = jax.nn.softmax(sim, axis=-1)
            out = jnp.einsum('bhwij,bhwjd->bhwid', attn, bv)
            return out.reshape(b, h, n, d)

        def _layer(x, wqkv, qs, ksc, wo, lg, lb, w1, b1, w2, b2):
            b, n, _ = x.shape
            h = shift_token(x)
            qkv = h @ wqkv
            q, k, v = jnp.split(qkv, 3, axis=-1)
            to_heads = lambda t: t.reshape(b, n, HEADS, DIM_HEAD).transpose(0, 2, 1, 3)
            q, k, v = (to_heads(q), to_heads(k), to_heads(v))
            q = l2norm(q) * qs
            k = l2norm(k) * ksc
            q, k = rotary_xpos(q, k)
            o = local_attention(q, k, v)
            o = o.transpose(0, 2, 1, 3).reshape(b, n, INNER)
            x = x + o @ wo
            h = shift_token(x)
            mu = h.mean(-1, keepdims=True)
            var = h.var(-1, keepdims=True)
            h = (h - mu) / jnp.sqrt(var + 1e-05) * lg + lb
            h = h @ w1 + b1
            a, g = jnp.split(h, 2, axis=-1)
            h = a * jax.nn.gelu(g, approximate=False)
            x = x + h @ w2 + b2
            return x
        key = jax.random.key(seed)
        ks = jax.random.split(key, 6)
        return {'x': jax.random.normal(ks[0], (B, N, DIM), jnp.float32), 'wqkv': jax.random.normal(ks[1], (DEPTH, DIM, 3 * INNER), jnp.float32) * 0.02, 'q_scale': jnp.ones((DEPTH, DIM_HEAD), jnp.float32), 'k_scale': jnp.ones((DEPTH, DIM_HEAD), jnp.float32), 'wo': jax.random.normal(ks[2], (DEPTH, INNER, DIM), jnp.float32) * 0.02, 'ln_g': jnp.ones((DEPTH, DIM), jnp.float32), 'ln_b': jnp.zeros((DEPTH, DIM), jnp.float32), 'w1': jax.random.normal(ks[3], (DEPTH, DIM, 2 * HID), jnp.float32) * 0.02, 'b1': jnp.zeros((DEPTH, 2 * HID), jnp.float32), 'w2': jax.random.normal(ks[4], (DEPTH, HID, DIM), jnp.float32) * 0.02, 'b2': jnp.zeros((DEPTH, DIM), jnp.float32)}
    _L3_ffn_in = _L3_ffn_setup()
    _d = {'L0_attn_query': _L0_attn_in['query'], 'L0_attn_in_proj_w': _L0_attn_in['in_proj_w'], 'L0_attn_out_proj_w': _L0_attn_in['out_proj_w'], 'L0_ffn_W_r': _L0_ffn_in['W_r'], 'L0_ffn_W_k': _L0_ffn_in['W_k'], 'L0_ffn_W_v': _L0_ffn_in['W_v'], 'L0_ffn_mu_r': _L0_ffn_in['mu_r'], 'L0_ffn_mu_k': _L0_ffn_in['mu_k'], 'L1_attn_Wq': _L1_attn_in['Wq'], 'L1_attn_bq': _L1_attn_in['bq'], 'L1_attn_Wk': _L1_attn_in['Wk'], 'L1_attn_bk': _L1_attn_in['bk'], 'L1_attn_Wv': _L1_attn_in['Wv'], 'L1_attn_bv': _L1_attn_in['bv'], 'L1_attn_Wo': _L1_attn_in['Wo'], 'L1_attn_bo': _L1_attn_in['bo'], 'L1_ffn_Wg': _L1_ffn_in['Wg'], 'L1_ffn_bg': _L1_ffn_in['bg'], 'L1_ffn_W1': _L1_ffn_in['W1'], 'L1_ffn_b1': _L1_ffn_in['b1'], 'L1_ffn_W2': _L1_ffn_in['W2'], 'L1_ffn_b2': _L1_ffn_in['b2'], 'L2_attn_Wq': _L2_attn_in['Wq'], 'L2_attn_bq': _L2_attn_in['bq'], 'L2_attn_Wk': _L2_attn_in['Wk'], 'L2_attn_bk': _L2_attn_in['bk'], 'L2_attn_Wv': _L2_attn_in['Wv'], 'L2_attn_bv': _L2_attn_in['bv'], 'L2_attn_Wo': _L2_attn_in['Wo'], 'L2_attn_bo': _L2_attn_in['bo'], 'L2_attn_W1': _L2_attn_in['W1'], 'L2_attn_b1': _L2_attn_in['b1'], 'L2_attn_W2': _L2_attn_in['W2'], 'L2_attn_b2': _L2_attn_in['b2'], 'L2_attn_g1': _L2_attn_in['g1'], 'L2_attn_beta1': _L2_attn_in['beta1'], 'L2_attn_g2': _L2_attn_in['g2'], 'L2_attn_beta2': _L2_attn_in['beta2'], 'L2_ffn_gate_w': _L2_ffn_in['gate_w'], 'L2_ffn_gate_b': _L2_ffn_in['gate_b'], 'L2_ffn_w1': _L2_ffn_in['w1'], 'L2_ffn_b1': _L2_ffn_in['b1'], 'L2_ffn_w2': _L2_ffn_in['w2'], 'L2_ffn_b2': _L2_ffn_in['b2'], 'L3_attn_ln_w': _L3_attn_in['ln_w'], 'L3_attn_ln_b': _L3_attn_in['ln_b'], 'L3_attn_in_proj_w': _L3_attn_in['in_proj_w'], 'L3_attn_conv_w': _L3_attn_in['conv_w'], 'L3_attn_conv_b': _L3_attn_in['conv_b'], 'L3_attn_dt_bias': _L3_attn_in['dt_bias'], 'L3_attn_A_log': _L3_attn_in['A_log'], 'L3_attn_Dvec': _L3_attn_in['Dvec'], 'L3_attn_rms_w': _L3_attn_in['rms_w'], 'L3_attn_out_proj_w': _L3_attn_in['out_proj_w'], 'L3_ffn_wqkv': _L3_ffn_in['wqkv'], 'L3_ffn_q_scale': _L3_ffn_in['q_scale'], 'L3_ffn_k_scale': _L3_ffn_in['k_scale'], 'L3_ffn_wo': _L3_ffn_in['wo'], 'L3_ffn_ln_g': _L3_ffn_in['ln_g'], 'L3_ffn_ln_b': _L3_ffn_in['ln_b'], 'L3_ffn_w1': _L3_ffn_in['w1'], 'L3_ffn_b1': _L3_ffn_in['b1'], 'L3_ffn_w2': _L3_ffn_in['w2'], 'L3_ffn_b2': _L3_ffn_in['b2']}
    _x0 = _d['L0_attn_query']
    _d['L0_attn_query'] = jax.random.normal(jax.random.fold_in(jax.random.key(seed), 1), (4, 1024, 128), dtype=_x0.dtype)
    del _x0
    return _d

def reference(L0_attn_query, L0_attn_in_proj_w, L0_attn_out_proj_w, L0_ffn_W_r, L0_ffn_W_k, L0_ffn_W_v, L0_ffn_mu_r, L0_ffn_mu_k, L1_attn_Wq, L1_attn_bq, L1_attn_Wk, L1_attn_bk, L1_attn_Wv, L1_attn_bv, L1_attn_Wo, L1_attn_bo, L1_ffn_Wg, L1_ffn_bg, L1_ffn_W1, L1_ffn_b1, L1_ffn_W2, L1_ffn_b2, L2_attn_Wq, L2_attn_bq, L2_attn_Wk, L2_attn_bk, L2_attn_Wv, L2_attn_bv, L2_attn_Wo, L2_attn_bo, L2_attn_W1, L2_attn_b1, L2_attn_W2, L2_attn_b2, L2_attn_g1, L2_attn_beta1, L2_attn_g2, L2_attn_beta2, L2_ffn_gate_w, L2_ffn_gate_b, L2_ffn_w1, L2_ffn_b1, L2_ffn_w2, L2_ffn_b2, L3_attn_ln_w, L3_attn_ln_b, L3_attn_in_proj_w, L3_attn_conv_w, L3_attn_conv_b, L3_attn_dt_bias, L3_attn_A_log, L3_attn_Dvec, L3_attn_rms_w, L3_attn_out_proj_w, L3_ffn_wqkv, L3_ffn_q_scale, L3_ffn_k_scale, L3_ffn_wo, L3_ffn_ln_g, L3_ffn_ln_b, L3_ffn_w1, L3_ffn_b1, L3_ffn_w2, L3_ffn_b2):

    def _L0_attn_ref(query, in_proj_w, out_proj_w):
        import jax, jax.numpy as jnp
        import numpy as np
        EMBED_DIM = 128
        NUM_HEADS = 16
        CONTEXT = 250
        MAX_PERIOD = 10000.0
        HEAD_DIM = EMBED_DIM // NUM_HEADS

        def _apply_rope(q, k):
            B, H, T, D = q.shape
            ds = jnp.arange(D // 2, dtype=jnp.float32)
            freqs = jnp.exp(ds * (-np.log(MAX_PERIOD) * 2.0 / D))
            ts = jnp.arange(T, dtype=jnp.float32)
            ang = ts[:, None] * freqs[None, :]
            cos = jnp.cos(ang)
            sin = jnp.sin(ang)

            def rot(x):
                xr = x.reshape(B, H, T, D // 2, 2)
                xa, xb = (xr[..., 0], xr[..., 1])
                ya = xa * cos - xb * sin
                yb = xa * sin + xb * cos
                return jnp.stack([ya, yb], axis=-1).reshape(B, H, T, D)
            return (rot(q), rot(k))
        B, T, E = query.shape
        H, D = (NUM_HEADS, HEAD_DIM)
        proj = query @ in_proj_w.T
        qkv = proj.reshape(B, T, 3, H, D)
        q = jnp.transpose(qkv[:, :, 0], (0, 2, 1, 3))
        k = jnp.transpose(qkv[:, :, 1], (0, 2, 1, 3))
        v = jnp.transpose(qkv[:, :, 2], (0, 2, 1, 3))
        q, k = _apply_rope(q, k)
        pos = jnp.arange(T)
        delta = pos[:, None] - pos[None, :]
        mask = (delta >= 0) & (delta < CONTEXT)
        scores = jnp.einsum('bhtd,bhsd->bhts', q, k) * D ** (-0.5)
        scores = jnp.where(mask[None, None, :, :], scores, jnp.finfo(scores.dtype).min)
        attn = jax.nn.softmax(scores, axis=-1)
        x = jnp.einsum('bhts,bhsd->bhtd', attn, v)
        x = jnp.transpose(x, (0, 2, 1, 3)).reshape(B, T, E)
        return x @ out_proj_w.T

    def _L0_ffn_ref(x, W_r, W_k, W_v, mu_r, mu_k):
        import jax, jax.numpy as jnp
        import numpy as np
        DIM = 128

        def _reference_tuple_inner(x, W_r, W_k, W_v, mu_r, mu_k):
            B, T, C = x.shape
            x_prev = jnp.concatenate([jnp.zeros((B, 1, C), x.dtype), x[:, :-1, :]], axis=1)
            xr = mu_r * x + (1.0 - mu_r) * x_prev
            xk = mu_k * x + (1.0 - mu_k) * x_prev
            r = jax.nn.sigmoid(jnp.einsum('btc,dc->btd', xr, W_r))
            k = jnp.einsum('btc,dc->btd', xk, W_k)
            k_act = jnp.square(jax.nn.relu(k))
            out = r * jnp.einsum('btc,dc->btd', k_act, W_v)
            new_state = x[:, -1, :]
            return (out, new_state)
        return _reference_tuple_inner(x, W_r, W_k, W_v, mu_r, mu_k)[0]

    def _L1_attn_ref(x, Wq, bq, Wk, bk, Wv, bv, Wo, bo):
        import jax, jax.numpy as jnp
        import numpy as np
        D_MODEL = 128
        N_HEADS = 16
        D_HEAD = D_MODEL // N_HEADS
        B, S, _ = x.shape

        def split_heads(t):
            return t.reshape(B, S, N_HEADS, D_HEAD).transpose(0, 2, 1, 3)
        Q = split_heads(x @ Wq + bq)
        K = split_heads(x @ Wk + bk)
        V = split_heads(x @ Wv + bv)
        scores = jnp.einsum('bhqd,bhkd->bhqk', Q, K)
        mask = jnp.tril(jnp.ones((S, S), dtype=bool))
        scores = jnp.where(mask[None, None], scores, jnp.float32(-1000000000.0))
        scores = scores / jnp.sqrt(jnp.float32(D_HEAD))
        attn = jax.nn.softmax(scores, axis=-1)
        ctx = jnp.einsum('bhqk,bhkd->bhqd', attn, V)
        ctx = ctx.transpose(0, 2, 1, 3).reshape(B, S, D_MODEL)
        return ctx @ Wo + bo

    def _L1_ffn_ref(x, Wg, bg, W1, b1, W2, b2):
        import jax, jax.numpy as jnp
        import numpy as np
        B, S, D, H, E, K = (4, 256, 128, 256, 8, 2)
        TEMP = 5.0
        EPS = 1e-09
        logits = jnp.einsum('bsd,de->bse', x, Wg) + bg
        probs = jax.nn.softmax(logits / TEMP, axis=-1)
        vals, idx = jax.lax.top_k(probs, K)
        onehot = jax.nn.one_hot(idx, E, dtype=x.dtype)
        mask = jnp.einsum('bske,bsk->bse', onehot, vals)
        gates = mask / (jnp.sum(mask, axis=-1, keepdims=True) + EPS)
        h = jax.nn.gelu(jnp.einsum('bsd,edh->besh', x, W1) + b1[None, :, None, :], approximate=False)
        out = jnp.einsum('besh,ehd->besd', h, W2) + b2[None, :, None, :]
        y = jnp.einsum('bse,besd->bsd', gates, out)
        return y

    def _L2_attn_ref(x, Wq, bq, Wk, bk, Wv, bv, Wo, bo, W1, b1, W2, b2, g1, beta1, g2, beta2):
        import jax, jax.numpy as jnp
        import numpy as np
        D_MODEL = 128
        NUM_HEADS = 16
        HEAD_DIM = D_MODEL // NUM_HEADS
        D_FF = 512
        EPS = 1e-05

        def layer_norm(x, gamma, beta):
            mu = jnp.mean(x, axis=-1, keepdims=True)
            var = jnp.mean((x - mu) ** 2, axis=-1, keepdims=True)
            return (x - mu) * jax.lax.rsqrt(var + EPS) * gamma + beta

        def apply_rope(t):
            S, d = (t.shape[-2], t.shape[-1])
            inv_freq = 1.0 / 10000.0 ** (jnp.arange(0, d, 2, dtype=jnp.float32) / d)
            angles = jnp.arange(S, dtype=jnp.float32)[:, None] * inv_freq[None, :]
            sin, cos = (jnp.sin(angles), jnp.cos(angles))
            tp = t.reshape(*t.shape[:-1], d // 2, 2)
            t0, t1 = (tp[..., 0], tp[..., 1])
            rot = jnp.stack([t0 * cos - t1 * sin, t0 * sin + t1 * cos], axis=-1)
            return rot.reshape(t.shape)
        B, S, d = x.shape
        H, hd = (NUM_HEADS, HEAD_DIM)
        x_norm = layer_norm(x, g1, beta1)
        q = (x_norm @ Wq + bq).reshape(B, S, H, hd).transpose(0, 2, 1, 3)
        k = (x_norm @ Wk + bk).reshape(B, S, H, hd).transpose(0, 2, 1, 3)
        v = (x_norm @ Wv + bv).reshape(B, S, H, hd).transpose(0, 2, 1, 3)
        q = apply_rope(q)
        k = apply_rope(k)
        q = q * (1.0 / jnp.sqrt(jnp.float32(hd)))
        scores = jnp.einsum('bhqd,bhkd->bhqk', q, k)
        attn = jax.nn.softmax(scores, axis=-1)
        out = jnp.einsum('bhqk,bhkd->bhqd', attn, v)
        out = out.transpose(0, 2, 1, 3).reshape(B, S, d)
        attn_out = out @ Wo + bo
        x = x + attn_out
        x_norm2 = layer_norm(x, g2, beta2)
        ffn = jax.nn.relu(x_norm2 @ W1 + b1) @ W2 + b2
        return x + ffn

    def _L2_ffn_ref(inputs, gate_w, gate_b, w1, b1, w2, b2):
        import jax, jax.numpy as jnp
        import numpy as np
        NUM_EXPERTS = 8
        CAPACITY = 80
        D = inputs.shape[-1]
        tokens = inputs.reshape(-1, D)
        logits = tokens @ gate_w + gate_b
        probs = jax.nn.softmax(logits, axis=-1)
        expert_idx = jnp.argmax(probs, axis=-1)
        mask1 = jax.nn.one_hot(expert_idx, NUM_EXPERTS, dtype=jnp.float32)
        pos = jnp.sum(jnp.cumsum(mask1, axis=0) * mask1, axis=-1) - 1.0
        pos = pos.astype(jnp.int32)
        keep = (pos < CAPACITY).astype(jnp.float32)
        gate_prob = jnp.sum(probs * mask1, axis=-1)
        pos_oh = jax.nn.one_hot(pos, CAPACITY, dtype=jnp.float32)
        sec_mask = mask1[:, :, None] * pos_oh[:, None, :] * keep[:, None, None]
        combine_weights = sec_mask * gate_prob[:, None, None]
        dispatch = jnp.einsum('nec,nd->ecd', sec_mask, tokens)
        h = jax.nn.gelu(jnp.einsum('ecd,edf->ecf', dispatch, w1) + b1[:, None, :])
        expert_out = jnp.einsum('ecf,efd->ecd', h, w2) + b2[:, None, :]
        out = jnp.einsum('nec,ecd->nd', combine_weights, expert_out)
        return out.reshape(inputs.shape)

    def _L3_attn_ref(h, ln_w, ln_b, in_proj_w, conv_w, conv_b, dt_bias, A_log, Dvec, rms_w, out_proj_w):
        import jax, jax.numpy as jnp
        import numpy as np
        from jax import lax
        C = 128
        D_STATE = 64
        D_CONV = 4
        EXPAND = 2
        HEADDIM = 64
        D_INNER = EXPAND * C
        NHEADS = D_INNER // HEADDIM
        NGROUPS = 1
        D_CONVDIM = D_INNER + 2 * NGROUPS * D_STATE
        D_INPROJ = 2 * D_INNER + 2 * NGROUPS * D_STATE + NHEADS
        EPS = 1e-05

        def _mamba_block(h, ln_w, ln_b, in_proj_w, conv_w, conv_b, dt_bias, A_log, Dvec, rms_w, out_proj_w):
            N, T, _ = h.shape
            res = h
            mu = jnp.mean(h, -1, keepdims=True)
            var = jnp.mean(jnp.square(h - mu), -1, keepdims=True)
            hn = (h - mu) * lax.rsqrt(var + EPS) * ln_w + ln_b
            zxbcdt = jnp.einsum('btc,dc->btd', hn, in_proj_w)
            z = zxbcdt[..., :D_INNER]
            xBC = zxbcdt[..., D_INNER:D_INNER + D_CONVDIM]
            dt = jax.nn.softplus(zxbcdt[..., D_INNER + D_CONVDIM:] + dt_bias)
            xp = jnp.pad(xBC, ((0, 0), (D_CONV - 1, 0), (0, 0)))
            conv = conv_b
            for k in range(D_CONV):
                conv = conv + xp[:, k:k + T, :] * conv_w[:, k]
            xBC = jax.nn.silu(conv)
            x = xBC[..., :D_INNER].reshape(N, T, NHEADS, HEADDIM)
            B = xBC[..., D_INNER:D_INNER + D_STATE]
            Cc = xBC[..., D_INNER + D_STATE:]
            A = -jnp.exp(A_log)
            dA = jnp.exp(dt * A)

            def step(state, inp):
                dA_t, dt_t, x_t, B_t, C_t = inp
                state = state * dA_t[:, :, None, None] + (dt_t[:, :, None] * x_t)[..., None] * B_t[:, None, None, :]
                y = jnp.einsum('bhpn,bn->bhp', state, C_t)
                return (state, y)
            xs = (jnp.moveaxis(dA, 1, 0), jnp.moveaxis(dt, 1, 0), jnp.moveaxis(x, 1, 0), jnp.moveaxis(B, 1, 0), jnp.moveaxis(Cc, 1, 0))
            state0 = jnp.zeros((N, NHEADS, HEADDIM, D_STATE), x.dtype)
            _, ys = lax.scan(step, state0, xs)
            y = jnp.moveaxis(ys, 0, 1) + Dvec[None, None, :, None] * x
            y = y.reshape(N, T, D_INNER)
            y = y * jax.nn.silu(z)
            y = y * lax.rsqrt(jnp.mean(jnp.square(y), -1, keepdims=True) + EPS) * rms_w
            out = jnp.einsum('btd,cd->btc', y, out_proj_w)
            return res + out
        return _mamba_block(h, ln_w, ln_b, in_proj_w, conv_w, conv_b, dt_bias, A_log, Dvec, rms_w, out_proj_w)

    def _L3_ffn_ref(x, wqkv, q_scale, k_scale, wo, ln_g, ln_b, w1, b1, w2, b2):
        import jax, jax.numpy as jnp
        import numpy as np
        DIM = 128
        DEPTH = 2
        HEADS = 8
        DIM_HEAD = 64
        WINDOW = 64
        INNER = HEADS * DIM_HEAD
        HID = int(DIM * 4 * 2 / 3)
        B, N = (2, 1024)
        QK_SCALE = 8.0

        def shift_token(t):
            t1, t2 = jnp.split(t, 2, axis=-1)
            t2 = jnp.pad(t2, ((0, 0), (1, 0), (0, 0)))[:, :-1]
            return jnp.concatenate([t1, t2], axis=-1)

        def l2norm(t):
            return t / jnp.clip(jnp.linalg.norm(t, axis=-1, keepdims=True), 1e-12)

        def rotate_half(x):
            x1, x2 = jnp.split(x, 2, axis=-1)
            return jnp.concatenate([-x2, x1], axis=-1)

        def rotary_xpos(q, k):
            n = q.shape[-2]
            half_idx = jnp.arange(0, DIM_HEAD, 2, dtype=jnp.float32)
            inv_freq = 1.0 / 10000.0 ** (half_idx / DIM_HEAD)
            t = jnp.arange(n, dtype=jnp.float32)
            freqs = t[:, None] * inv_freq[None, :]
            freqs = jnp.concatenate([freqs, freqs], axis=-1)
            base = (half_idx + 0.4 * DIM_HEAD) / (1.4 * DIM_HEAD)
            power = (t - n // 2) / float(WINDOW // 2)
            scale = base[None, :] ** power[:, None]
            scale = jnp.concatenate([scale, scale], axis=-1)
            cos, sin = (jnp.cos(freqs), jnp.sin(freqs))
            q = q * cos * scale + rotate_half(q) * sin * scale
            k = k * cos / scale + rotate_half(k) * sin / scale
            return (q, k)

        def local_attention(q, k, v):
            b, h, n, d = q.shape
            w = n // WINDOW
            bq = q.reshape(b, h, w, WINDOW, d) * QK_SCALE
            bk = k.reshape(b, h, w, WINDOW, d)
            bv = v.reshape(b, h, w, WINDOW, d)

            def look_around(t):
                p = jnp.pad(t, ((0, 0), (0, 0), (1, 0), (0, 0), (0, 0)))
                return jnp.concatenate([p[:, :, :w], p[:, :, 1:]], axis=3)
            bk, bv = (look_around(bk), look_around(bv))
            bt = jnp.arange(n).reshape(w, WINDOW)
            btp = jnp.pad(bt, ((1, 0), (0, 0)), constant_values=-1)
            btk = jnp.concatenate([btp[:w], btp[1:]], axis=1)
            sim = jnp.einsum('bhwid,bhwjd->bhwij', bq, bk)
            i = bt[:, :, None]
            j = btk[:, None, :]
            mask = (i < j) | (i > j + WINDOW) | (j == -1)
            sim = jnp.where(mask, -jnp.finfo(sim.dtype).max, sim)
            attn = jax.nn.softmax(sim, axis=-1)
            out = jnp.einsum('bhwij,bhwjd->bhwid', attn, bv)
            return out.reshape(b, h, n, d)

        def _layer(x, wqkv, qs, ksc, wo, lg, lb, w1, b1, w2, b2):
            b, n, _ = x.shape
            h = shift_token(x)
            qkv = h @ wqkv
            q, k, v = jnp.split(qkv, 3, axis=-1)
            to_heads = lambda t: t.reshape(b, n, HEADS, DIM_HEAD).transpose(0, 2, 1, 3)
            q, k, v = (to_heads(q), to_heads(k), to_heads(v))
            q = l2norm(q) * qs
            k = l2norm(k) * ksc
            q, k = rotary_xpos(q, k)
            o = local_attention(q, k, v)
            o = o.transpose(0, 2, 1, 3).reshape(b, n, INNER)
            x = x + o @ wo
            h = shift_token(x)
            mu = h.mean(-1, keepdims=True)
            var = h.var(-1, keepdims=True)
            h = (h - mu) / jnp.sqrt(var + 1e-05) * lg + lb
            h = h @ w1 + b1
            a, g = jnp.split(h, 2, axis=-1)
            h = a * jax.nn.gelu(g, approximate=False)
            x = x + h @ w2 + b2
            return x
        for l in range(DEPTH):
            x = _layer(x, wqkv[l], q_scale[l], k_scale[l], wo[l], ln_g[l], ln_b[l], w1[l], b1[l], w2[l], b2[l])
        return x
    x = L0_attn_query
    xn = _layernorm(x, axis=-1)
    s = _L0_attn_ref(xn, L0_attn_in_proj_w, L0_attn_out_proj_w)
    g = _silu(_L0_ffn_ref(xn, L0_ffn_W_r, L0_ffn_W_k, L0_ffn_W_v, L0_ffn_mu_r, L0_ffn_mu_k))
    x = x + s * g
    xn = _layernorm(x, axis=-1)
    s = _L1_attn_ref(xn, L1_attn_Wq, L1_attn_bq, L1_attn_Wk, L1_attn_bk, L1_attn_Wv, L1_attn_bv, L1_attn_Wo, L1_attn_bo)
    g = _silu(_L1_ffn_ref(xn, L1_ffn_Wg, L1_ffn_bg, L1_ffn_W1, L1_ffn_b1, L1_ffn_W2, L1_ffn_b2))
    x = x + s * g
    xn = _layernorm(x, axis=-1)
    s = _L2_attn_ref(xn, L2_attn_Wq, L2_attn_bq, L2_attn_Wk, L2_attn_bk, L2_attn_Wv, L2_attn_bv, L2_attn_Wo, L2_attn_bo, L2_attn_W1, L2_attn_b1, L2_attn_W2, L2_attn_b2, L2_attn_g1, L2_attn_beta1, L2_attn_g2, L2_attn_beta2)
    g = _silu(_L2_ffn_ref(xn, L2_ffn_gate_w, L2_ffn_gate_b, L2_ffn_w1, L2_ffn_b1, L2_ffn_w2, L2_ffn_b2))
    x = x + s * g
    xn = _layernorm(x, axis=-1)
    s = _L3_attn_ref(xn, L3_attn_ln_w, L3_attn_ln_b, L3_attn_in_proj_w, L3_attn_conv_w, L3_attn_conv_b, L3_attn_dt_bias, L3_attn_A_log, L3_attn_Dvec, L3_attn_rms_w, L3_attn_out_proj_w)
    g = _silu(_L3_ffn_ref(xn, L3_ffn_wqkv, L3_ffn_q_scale, L3_ffn_k_scale, L3_ffn_wo, L3_ffn_ln_g, L3_ffn_ln_b, L3_ffn_w1, L3_ffn_b1, L3_ffn_w2, L3_ffn_b2))
    x = x + s * g
    return x

_drawn_inputs = setup_inputs


def setup_inputs(seed=0):
    import zlib

    import numpy as np

    out = dict(_drawn_inputs(seed))
    spreads = {'L1_attn_bq': (0.0, 0.1),
     'L1_attn_bk': (0.0, 0.1),
     'L1_attn_bv': (0.0, 0.1),
     'L1_attn_bo': (0.0, 0.1),
     'L1_ffn_bg': (0.0, 0.1),
     'L1_ffn_b1': (0.0, 0.1),
     'L1_ffn_b2': (0.0, 0.1),
     'L2_attn_bq': (0.0, 0.1),
     'L2_attn_bk': (0.0, 0.1),
     'L2_attn_bv': (0.0, 0.1),
     'L2_attn_bo': (0.0, 0.1),
     'L2_attn_b1': (0.0, 0.1),
     'L2_attn_b2': (0.0, 0.1),
     'L2_attn_g1': (1.0, 0.2),
     'L2_attn_beta1': (0.0, 0.1),
     'L2_attn_g2': (1.0, 0.2),
     'L2_attn_beta2': (0.0, 0.1),
     'L2_ffn_gate_b': (0.0, 0.1),
     'L2_ffn_b1': (0.0, 0.1),
     'L2_ffn_b2': (0.0, 0.1),
     'L3_attn_ln_w': (1.0, 0.2),
     'L3_attn_ln_b': (0.0, 0.1),
     'L3_attn_conv_b': (0.0, 0.1),
     'L3_attn_Dvec': (1.0, 0.2),
     'L3_attn_rms_w': (1.0, 0.2),
     'L3_ffn_q_scale': (1.0, 0.2),
     'L3_ffn_k_scale': (1.0, 0.2),
     'L3_ffn_ln_g': (1.0, 0.2),
     'L3_ffn_ln_b': (0.0, 0.1),
     'L3_ffn_b1': (0.0, 0.1),
     'L3_ffn_b2': (0.0, 0.1)}
    factors = {}
    for name, (base, spread) in spreads.items():
        noise = np.random.default_rng([zlib.crc32(name.encode()), seed]).standard_normal(out[name].shape)
        drawn = base * np.exp(spread * noise) if base else spread * noise
        out[name] = jnp.asarray(drawn.astype(out[name].dtype))
    for name, factor in factors.items():
        out[name] = (out[name] * factor).astype(out[name].dtype)
    return out
```

```python
from contextlib import ExitStack, contextmanager

import numpy as np

import concourse.bass as bass
from concourse import mybir

F32 = mybir.dt.float32
BF16 = mybir.dt.bfloat16
U32 = mybir.dt.uint32
ALU = mybir.AluOpType
ACT = mybir.ActivationFunctionType
AX = mybir.AxisListType

B, T, C = 4, 1024, 128
P = 128
NT = T // P
HALF = 512
NH, DH = 16, 8
GH = 4
NG = NH // GH
EPS = 1e-5
BIG = 1e30
CONTEXT = 250
EDGE = 2 * P - CONTEXT


def pack_columns(parts):
    where, at = {}, 0
    for name, a in parts:
        where[name] = (at, a.shape[1], a.shape[0])
        at += a.shape[1]
    out = np.zeros((P, at), np.float32)
    for name, a in parts:
        o, n, r = where[name]
        out[:r, o:o + n] = a
    return out, where


def row(v):
    return np.broadcast_to(np.asarray(v).reshape(1, -1), (P, np.asarray(v).size))


def cols(v, n=1):
    v = np.asarray(v).reshape(-1)
    out = np.zeros((P, n), np.float32)
    for i in range(n):
        piece = v[i * P:(i + 1) * P]
        out[:piece.size, i] = piece
    return out


def kblocks(w, kb=P):
    w = np.asarray(w)
    nb = -(-w.shape[0] // kb)
    out = np.zeros((P, nb * w.shape[1]), np.float32)
    for j in range(nb):
        piece = w[j * kb:(j + 1) * kb]
        out[:piece.shape[0], j * w.shape[1]:(j + 1) * w.shape[1]] = piece
    return out


SWAP = np.arange(C) ^ 1


def weights_of(i):
    g = {k: np.asarray(v) for k, v in i.items()}
    ipw = g["L0_attn_in_proj_w"]
    l0 = []
    for n, j in (("q", 0), ("k", 1)):
        w = ipw[j * C:(j + 1) * C].T
        l0 += [("l0_w" + n, w), ("l0_w" + n + "s", w[:, SWAP])]
    l0 += [("l0_wv", ipw[2 * C:].T), ("l0_wo", g["L0_attn_out_proj_w"].T),
           ("l0_r", g["L0_ffn_W_r"].T), ("l0_k", g["L0_ffn_W_k"].T), ("l0_v", g["L0_ffn_W_v"].T),
           ("l0_mu_r", cols(g["L0_ffn_mu_r"])), ("l0_mu_k", cols(g["L0_ffn_mu_k"]))]
    l1 = [("l1_w" + n, g["L1_attn_W" + n]) for n in "qkvo"]
    l1 += [("l1_bq", cols(g["L1_attn_bq"])), ("l1_bk", cols(g["L1_attn_bk"])),
           ("l1_bv", row(g["L1_attn_bv"])), ("l1_bo", row(g["L1_attn_bo"])),
           ("l1_wg", g["L1_ffn_Wg"]), ("l1_bg", row(g["L1_ffn_bg"]))]
    for e in range(8):
        l1 += [(f"l1_w1_{e}", g["L1_ffn_W1"][e]), (f"l1_b1_{e}", cols(g["L1_ffn_b1"][e], 2)),
               (f"l1_w2_{e}", kblocks(g["L1_ffn_W2"][e]))]
    l1 += [("l1_b2", g["L1_ffn_b2"])]
    l2 = []
    for n in "qk":
        w, b = g["L2_attn_W" + n], g["L2_attn_b" + n]
        l2 += [("l2_w" + n, w), ("l2_w" + n + "s", w[:, SWAP]), ("l2_b" + n, cols(b)), ("l2_b" + n + "s", cols(b[SWAP]))]
    l2 += [("l2_wv", g["L2_attn_Wv"]), ("l2_wo", g["L2_attn_Wo"]),
           ("l2_bv", row(g["L2_attn_bv"])), ("l2_bo", row(g["L2_attn_bo"])),
           ("l2_g1", cols(g["L2_attn_g1"])), ("l2_be1", cols(g["L2_attn_beta1"])),
           ("l2_g2", cols(g["L2_attn_g2"])), ("l2_be2", cols(g["L2_attn_beta2"])),
           ("l2_w1", g["L2_attn_W1"]), ("l2_b1", cols(g["L2_attn_b1"], 4)),
           ("l2_w2", kblocks(g["L2_attn_W2"])), ("l2_b2", row(g["L2_attn_b2"])),
           ("l2_gw", g["L2_ffn_gate_w"]), ("l2_gb", row(g["L2_ffn_gate_b"])),
           ("l2_eb1", np.concatenate([cols(g["L2_ffn_b1"][e], 4) for e in range(8)], 1))]
    wi = g["L3_attn_in_proj_w"].T
    cw, cb = g["L3_attn_conv_w"], g["L3_attn_conv_b"]
    l3 = [("l3_lnw", cols(g["L3_attn_ln_w"])), ("l3_lnb", cols(g["L3_attn_ln_b"])),
          ("l3_z", wi[:, 0:256]), ("l3_xbc", wi[:, 256:640]), ("l3_dt", wi[:, 640:644])]
    for j, (a, e) in enumerate(((0, 128), (128, 256), (256, 320), (320, 384))):
        l3 += [(f"l3_cw{j}", cw[a:e]), (f"l3_cb{j}", cb[a:e].reshape(-1, 1))]
    l3 += [("l3_dtb", row(g["L3_attn_dt_bias"])), ("l3_alog", row(g["L3_attn_A_log"])),
           ("l3_dv", row(g["L3_attn_Dvec"])), ("l3_rms", row(g["L3_attn_rms_w"])),
           ("l3_out", kblocks(g["L3_attn_out_proj_w"].T))]
    for d in range(2):
        w1 = g["L3_ffn_w1"][d]
        b1 = g["L3_ffn_b1"][d]
        hid = w1.shape[1] // 2
        l3 += [(f"l3_wqkv{d}", g["L3_ffn_wqkv"][d]), (f"l3_qs{d}", row(g["L3_ffn_q_scale"][d])),
               (f"l3_ks{d}", row(g["L3_ffn_k_scale"][d])), (f"l3_wo{d}", kblocks(g["L3_ffn_wo"][d])),
               (f"l3_lg{d}", cols(g["L3_ffn_ln_g"][d])), (f"l3_lb{d}", cols(g["L3_ffn_ln_b"][d])),
               (f"l3_w1{d}", w1), (f"l3_b1a{d}", cols(b1[:hid], 3)), (f"l3_b1g{d}", cols(b1[hid:], 3)),
               (f"l3_w2{d}", kblocks(g["L3_ffn_w2"][d])), (f"l3_b2{d}", row(g["L3_ffn_b2"][d]))]
    return [l0, l1, l2, l3]


def switch_weights_of(i):
    w1, w2, b2 = (np.asarray(i["L2_ffn_" + n]) for n in ("w1", "w2", "b2"))
    return [("w1", np.concatenate([w1[e] for e in range(8)], 1)),
            ("w2", np.concatenate([kblocks(w2[e]) for e in range(8)], 1)),
            ("b2", np.concatenate([row(b2[e]) for e in range(8)], 1))]


def constants():
    q, k = np.arange(P)[:, None], np.arange(P)[None, :]
    later = np.where(k > q, -BIG, 0.0)
    far1 = np.where(P + q - k >= CONTEXT, -BIG, 0.0)
    far2 = np.where(2 * P + q - k >= CONTEXT, -BIG, 0.0)
    parts = [("ident", np.eye(P)), ("later_qk", later), ("later_kq", later.T),
             ("band_qk", np.concatenate([far2, far1, later], 1)),
             ("band_kq", np.concatenate([later.T, far1.T, far2.T], 1))]
    d = np.arange(C) % DH // 2
    ang = np.arange(T)[None, :] * (10000.0 ** (-2.0 * d / DH))[:, None]
    sign = np.where(np.arange(C) % 2 == 0, -1.0, 1.0)[:, None]
    parts += [("rope_cos", np.cos(ang)), ("rope_sin", sign * np.sin(ang))]
    D, W = 64, 64
    half = np.arange(0, D, 2)
    fr = np.arange(T)[:, None] / 10000.0 ** (half / D)[None, :]
    sc = ((half + 0.4 * D) / (1.4 * D))[None, :] ** ((np.arange(T) - T // 2) / (W // 2))[:, None]
    two = lambda a: np.concatenate([a, a], 1)
    sgn = np.concatenate([-np.ones(D // 2), np.ones(D // 2)])[None, :]
    tile = lambda a: a.reshape(NT, P, D).transpose(1, 0, 2).reshape(P, NT * D)
    parts += [("xq_cos", tile(two(np.cos(fr) * sc * 8))), ("xq_sin", tile(two(np.sin(fr) * sc * 8) * sgn)),
              ("xk_cos", tile(two(np.cos(fr) / sc))), ("xk_sin", tile(two(np.sin(fr) / sc) * sgn))]
    k2 = np.arange(2 * P)[None, :] - P
    parts += [("local_qk", np.where((k2 > q) | (q - k2 > 64), -BIG, 0.0)),
              ("shift", (k == q + 1) * 1.0), ("carry", ((q == P - 1) & (k == 0)) * 1.0), ("tri", (q <= k) * 1.0), ("ones", np.ones((P, P))),
              ("iota8", row(np.arange(8))), ("iota640", row(np.arange(640))),
              ("slot_id", (np.arange(P)[:, None] + 80 * np.arange(8)[None, :]) * 1.0)]
    return [(n, np.asarray(a, np.float64).astype(np.float32)) for n, a in parts]


class Net:

    def __init__(self, nc, ctx):
        self.nc, self.ctx = nc, ctx
        self.stale_next, self.sems_before = [], None
        self.early = {n: ctx.enter_context(nc.semaphore(n)) for n in ("stored", "stack0", "ones")}

    def sbuf(self, name, shape, dt=F32):
        return self.ctx.enter_context(self.nc.sbuf_tensor(name, shape, dt))

    @contextmanager
    def phase(self, kind, names):
        self.n += 1
        sems, mem = ExitStack(), ExitStack()
        S = {n: sems.enter_context(self.nc.semaphore(f"{kind}_{n}_{self.n}")) for n in names}
        self.stale, before = self.stale_next, self.sems_before
        self.stale_next, self.sems_before = list(S.values()), sems
        with mem:
            self.mem = mem
            yield S, self.nc.Block(no_gpsimd_drain=True)
        if before is not None:
            before.close()

    def end_of_row(self):
        self.sems_before.close()
        self.stale_next, self.sems_before = [], None

    n = 0

    def tmp(self, name, shape, dt=F32):
        return self.mem.enter_context(self.nc.sbuf_tensor(f"{name}_{self.n}", shape, dt))

    def psum(self, name, shape, dt=F32):
        return self.mem.enter_context(self.nc.psum_tensor(f"{name}_{self.n}", shape, dt))

    def clear_previous(self, sp):
        for s in self.stale:
            sp.sem_clear(s)


def load_constants(net):
    nc = net.nc
    with net.phase("load", ["landed", "done"]) as (S, blk), blk as block:
        @block.sync
        def _(sp):
            for dst, src in net.loads:
                sp.dma_start(dst, src).then_inc(S["landed"], 16)
            sp.wait_ge(S["landed"], 16 * len(net.loads))

        @block.vector
        def _(dve):
            dve.wait_ge(S["landed"], 16 * len(net.loads))
            for dst, src in net.casts:
                nc.vector.tensor_copy(dst, src).then_inc(S["done"], 1)
            nc.vector.memset(net.zeros_bf[:, :], 0.0).then_inc(S["done"], 1)
            nc.vector.memset(net.count[:, :], 0.0).then_inc(S["done"], 1)


def layer_norm(net, src, dst_tok=None, dst_ch=None, gamma=None, beta=None, load=None):
    nc = net.nc
    with net.phase("ln", ["landed", "stat", "var", "std", "rstd", "norm", "turned"]) as (S, blk):
        st = net.tmp("st", [P, NT, 6])
        mv = net.tmp("mv", [P, NT, 2])
        std = net.tmp("std", [P, NT])
        rstd = net.tmp("rstd", [P, NT])
        out = net.tmp("nrm", [P, NT, C]) if dst_tok is None else dst_tok
        turn = net.psum("turn", [P, 2, HALF])
        with blk as block:
            @block.sync
            def _(sp):
                net.clear_previous(sp)
                if load is not None:
                    sp.dma_start(src[:, :, :], load).then_inc(S["landed"], 16)

            @block.vector
            def _(dve):
                if load is not None:
                    dve.wait_ge(S["landed"], 16)
                for t in range(NT):
                    nc.vector.bn_stats(st[:, t, :], src[:, t, :]).then_inc(S["stat"], 1)
                for t in range(NT):
                    dve.wait_ge(S["stat"], t + 1)
                    nc.vector.bn_aggr(mv[:, t, :], st[:, t, :]).then_inc(S["var"], 1)
                dve.wait_ge(S["var"], NT)
                nc.vector.tensor_scalar(std[:, :], mv[:, :, 1], EPS, None, ALU.add).then_inc(S["var"], 1)
                dve.wait_ge(S["std"], 1)
                nc.vector.reciprocal(rstd[:, :], std[:, :]).then_inc(S["rstd"], 1)
                dve.wait_ge(S["rstd"], 1)
                for t in range(NT):
                    nc.vector.tensor_scalar(out[:, t, :], src[:, t, :], mv[:, t, 0:1], rstd[:, t:t + 1],
                                            ALU.subtract, ALU.mult).then_inc(S["norm"], 1)

            @block.scalar
            def _(act):
                act.wait_ge(S["var"], NT + 1)
                nc.scalar.activation(std[:, :], std[:, :], ACT.Sqrt).then_inc(S["std"], 1)
                if dst_ch is not None:
                    for i in range(2):
                        act.wait_ge(S["turned"], i + 1)
                        if gamma is None:
                            nc.scalar.activation(dst_ch[:, i * HALF:(i + 1) * HALF], turn[:, i, :], ACT.Identity)
                        else:
                            nc.scalar.activation(dst_ch[:, i * HALF:(i + 1) * HALF], turn[:, i, :], ACT.Identity,
                                                 scale=gamma, bias=beta)

            @block.tensor
            def _(pe):
                if dst_ch is not None:
                    for t in range(NT):
                        pe.wait_ge(S["norm"], t + 1)
                        last = nc.tensor.transpose(turn[:, t // 4, t % 4 * P:(t % 4 + 1) * P], out[:, t, :], net.ident)
                        if t % 4 == 3:
                            last.then_inc(S["turned"], 1)


@contextmanager
def attention_inputs(net):
    with ExitStack() as keep:
        net.qs0 = keep.enter_context(net.nc.sbuf_tensor(f"qs0_{net.n}", [P, GH, T], BF16))
        net.ks0 = keep.enter_context(net.nc.sbuf_tensor(f"ks0_{net.n}", [P, GH, T], BF16))
        net.part_mem = keep.enter_context(ExitStack())
        net.part = net.part_mem.enter_context(net.nc.sbuf_tensor(f"part_{net.n}", [P, 2, 3, T], BF16))
        yield


def load_stacks(net, sp, g, qs, ks, landed):
    for r in range(3):
        sp.dma_start(qs[24 * r:24 * r + 24, :, :],
                     net.q_scr[GH * g:GH * g + GH].rearrange("h a d t -> (a d) h t")).then_inc(landed, 16)
        sp.dma_start(ks[24 * r:24 * r + 24, :, :],
                     net.k_scr[GH * g:GH * g + GH, r:r + 3].rearrange("h a d t -> (a d) h t")).then_inc(landed, 16)


def store_keys(net, sp):
    for a in range(5):
        sp.dma_start(net.k_scr[:, a], net.part[:, 1, a % 3, :]).then_inc(net.early["stored"], 16)


def load_first_stacks(net, sp):
    sp.wait_ge(net.early["ones"], 1)
    sp.wait_ge(net.early["stored"], 16 * STORES)
    load_stacks(net, sp, 0, net.qs0, net.ks0, net.early["stack0"])


STORES = 3 + 5


def project_qkv(net, src_ch, w, bias=None, bias_s=None, rope=False):
    nc = net.nc
    units = [(m, c) for m in range(2) for c in range(2)]
    with net.phase("qkv", ["product", "used", "value", "c", "s", "sum", "p1", "r1", "p2", "p3", "vmm", "vout"]) as (S, blk):
        pa = net.psum("pa", [P, 2, HALF])
        pb = net.psum("pb", [P, 2, HALF])
        pv = net.psum("pv", [P, 2, HALF])
        ta = net.tmp("ta", [P, 2, HALF])
        tb = net.tmp("tb", [P, 2, HALF])
        rest = net.tmp("rest", [P, 2, HALF])
        part = net.part
        with blk as block:
            @block.tensor
            def _(pe):
                for u, (m, c) in enumerate(units):
                    x = src_ch[:, c * HALF:(c + 1) * HALF]
                    if u >= 2:
                        pe.wait_ge(S["value"], u - 1)
                    last = nc.tensor.matmul(pa[:, u % 2, :], w["qk"[m]], x, start=True, stop=True)
                    if rope:
                        last = nc.tensor.matmul(pb[:, u % 2, :], w["qk"[m] + "s"], x, start=True, stop=True)
                    last.then_inc(S["product"], 1)
                for t in range(NT):
                    last = nc.tensor.matmul(pv[:, t // 4, t % 4 * C:(t % 4 + 1) * C], src_ch[:, t * P:(t + 1) * P],
                                            w["v"], start=True, stop=True)
                    if t % 4 == 3:
                        last.then_inc(S["vmm"], 1)

            @block.vector
            def _(dve):
                def value(u):
                    m, c = units[u]
                    cs = slice(c * HALF, (c + 1) * HALF)
                    dve.wait_ge(S["product"], u + 1)
                    if u >= 2:
                        dve.wait_ge(S["p1"], u - 1)
                        dve.wait_ge(S["p3"], u - 1)
                    if rope:
                        bq = 0.0 if bias is None else bias["qk"[m]]
                        bs = 0.0 if bias_s is None else bias_s["qk"[m]]
                        nc.vector.scalar_tensor_tensor(out=tb[:, u % 2, :], in0=pb[:, u % 2, :], scalar=bs,
                                                       in1=net.rope_sin[:, cs], op0=ALU.add, op1=ALU.mult).then_inc(S["s"], 1)
                        nc.vector.scalar_tensor_tensor(out=rest[:, u % 2, :], in0=pa[:, u % 2, :], scalar=bq,
                                                       in1=net.rope_cos[:, cs], op0=ALU.add, op1=ALU.mult).then_inc(S["value"], 1)
                        dve.wait_ge(S["s"], u + 1)
                        dve.wait_ge(S["value"], u + 1)
                        nc.vector.tensor_tensor(ta[:, u % 2, :], rest[:, u % 2, :], tb[:, u % 2, :], ALU.add).then_inc(S["sum"], 1)
                    else:
                        nc.vector.tensor_scalar(ta[:, u % 2, :], pa[:, u % 2, :], bias["qk"[m]], None,
                                                ALU.add).then_inc(S["value"], 1)

                for m in range(2):
                    for c in range(2):
                        value(2 * m + c)
                    for c in range(2):
                        u, cs = 2 * m + c, slice(c * HALF, (c + 1) * HALF)
                        dve.wait_ge(S["p1"], u + 1)
                        nc.vector.tensor_tensor(rest[:, c, :], ta[:, c, :], part[:, m, 0, cs], ALU.subtract).then_inc(S["r1"], 1)
                    for c in range(2):
                        u, cs = 2 * m + c, slice(c * HALF, (c + 1) * HALF)
                        dve.wait_ge(S["p2"], u + 1)
                        nc.vector.tensor_tensor(part[:, m, 2, cs], rest[:, c, :], part[:, m, 1, cs], ALU.subtract).then_inc(S["p3"], 1)
                for i in range(2):
                    dve.wait_ge(S["vmm"], i + 1)
                    dst = net.v_tok[:, 4 * i:4 * i + 4, :]
                    src = pv[:, i, :].rearrange("p (t c) -> p t c", t=4)
                    if bias is None or "v" not in bias:
                        nc.vector.tensor_copy(dst, src).then_inc(S["vout"], 1)
                    else:
                        nc.vector.tensor_tensor(dst, src, bias["v"].unsqueeze(1).broadcast_to([P, 4, C]), ALU.add).then_inc(S["vout"], 1)

            @block.scalar
            def _(act):
                for m in range(2):
                    for c in range(2):
                        u, cs = 2 * m + c, slice(c * HALF, (c + 1) * HALF)
                        act.wait_ge(S["sum" if rope else "value"], u + 1)
                        nc.scalar.activation(part[:, m, 0, cs], ta[:, c, :], ACT.Copy).then_inc(S["p1"], 1)
                    for c in range(2):
                        u, cs = 2 * m + c, slice(c * HALF, (c + 1) * HALF)
                        act.wait_ge(S["r1"], u + 1)
                        nc.scalar.activation(part[:, m, 1, cs], rest[:, c, :], ACT.Copy).then_inc(S["p2"], 1)

            @block.sync
            def _(sp):
                net.clear_previous(sp)
                sp.wait_ge(S["p3"], 2)
                for a in range(3):
                    sp.dma_start(net.q_scr[:, a], part[:, 0, a, :]).then_inc(net.early["stored"], 16)

            @block.gpsimd
            def _(pool):
                nc.gpsimd.memset(net.ks0[64:96, :, :].bitcast(U32), 0x3F803F80).then_inc(net.early["ones"], 1)
                pool.wait_ge(net.early["ones"], 1)


def attention(net, mode, scale):
    nc = net.nc
    R = 9 * DH
    KR = R + 3

    def keys_of(t):
        return {"full": (0, T), "causal": (0, (t + 1) * P), "band": (max(0, t - 2) * P, (t + 1) * P)}[mode]

    def queries_of(kt):
        return {"full": (0, T), "causal": (kt * P, T), "band": (kt * P, min(kt + 3, NT) * P)}[mode]

    def split(lo, hi, at):
        out = []
        while lo < hi:
            nxt = min(hi, (lo // at + 1) * at)
            out.append((lo, nxt))
            lo = nxt
        return out

    steps = NT * GH

    def max_units(g):
        out = []
        for h in range(GH):
            for t in range(NT):
                lo, hi = keys_of(t)
                for i, k0 in enumerate(range(lo, hi, HALF)):
                    out.append(("max", g, h, t, k0, min(hi, k0 + HALF), i))
        return out

    lag = 1
    quarters = [[] for _ in range(NT * GH)]
    for kt in range(NT):
        pieces = split(*queries_of(kt), HALF)
        for j, piece in enumerate(pieces):
            quarters[kt * GH + j * GH // len(pieces)].append((kt, *piece))

    cost = []
    for i in range(steps):
        lo, hi = queries_of(i // GH)
        cost += [hi - lo, sum(q1 - q0 for _, q0, q1 in quarters[i - lag - GH])]
    landed_at, ready_at = {"band": (0.12, 0.9), "causal": (0.2, 0.95), "full": (0.15, 0.9)}[mode]
    until = sum(cost) * ready_at
    side = {(-1, 0, 0): max_units(0) + [("turn_max", 0)]}
    for g in range(NG):
        start = sum(cost) * landed_at if g >= 1 else 0
        units = max_units(g + 1) + [("turn_max", g + 1)] if g + 1 < NG else []
        if g >= 1:
            units[3:3] = [("turn_out", g - 1, 0), ("turn_out", g - 1, 1)]
            if not units[5:]:
                units = [None] * 8 + units
        spent, n = 0, 0
        for p, c in enumerate(cost):
            spent += c
            while n < len(units) and n < (spent - start) / (until - start) * len(units):
                if units[n] and not (units[n][0] == "turn_out" and p < 2 * (GH + lag) + 2):
                    side.setdefault((g, p // 2, p % 2), []).append(units[n])
                elif units[n]:
                    break
                n += 1
        for u in units[n:]:
            side.setdefault((g, steps - 1, 1), []).append(u)
    side[(NG, 0, 0)] = [("turn_out", NG - 1, 0), ("turn_out", NG - 1, 1)]
    order = [(-1, 0, 0)] + [(g, i, j) for g in range(NG) for i in range(steps) for j in range(2)] + [(NG, 0, 0)]

    with net.phase("att", ["stack1", "neg_landed", "mx_full", "mx_used", "combined", "neg", "neg_step", "scores", "exped",
                           "summed", "o_copied", "v_ready", "v_init", "init", "recip"]) as (S, blk):
        net.part_mem.close()
        net.stale_next = net.stale_next + list(net.early.values())
        qs = [net.qs0, net.tmp("qs1", [P, GH, T], BF16)]
        ks = [net.ks0, net.tmp("ks1", [P, GH, T], BF16)]
        prob = net.tmp("prob", [P, 2, GH, T])
        vst = net.tmp("vst", [P, 2, NT, GH, 32])
        mhalf = net.tmp("mhalf", [P, GH * NT, 2])
        mrow = net.tmp("mrow", [P, GH * NT])
        neg = net.tmp("neg", [GH * NT, 2, 3, P], BF16)
        nrest = net.tmp("nrest", [GH * NT, P])
        osb = net.tmp("osb", [P, T])
        rec = net.tmp("rec", [P, 4, GH])
        ps_st = net.psum("ps_st", [P, 2, T])
        ps_o = net.psum("ps_o", [P, T])
        mx = net.psum("mx", [P, 2, HALF])
        first = len(max_units(0))

        def bank_of(i):
            return ps_st[:, i // 2 % 2, i % 2 * HALF:(i % 2 + 1) * HALF] if i < first else mx[:, i % 2, :]

        stack = [net.early["stack0"], S["stack1"]]
        last_of = [max(k for k in range(NT) if queries_of(k)[0] < (i + 1) * HALF) for i in range(2)]

        with blk as block:
            def neg_rows(sp, g):
                sp.wait_ge(S["neg"], g + 1)
                for a in range(3):
                    sp.dma_start(qs[g % 2][R + a:R + a + 1, :, :], neg[:, g % 2, a, :]).then_inc(S["neg_landed"], 16)

            turned_before, seen = {}, 0
            for key in order:
                for u in side.get(key, []):
                    seen += 1
                    if u[0] == "turn_out":
                        turned_before[u[1] + 1] = seen

            @block.sync
            def _(sp):
                net.clear_previous(sp)
                sp.wait_ge(S["init"], 1)
                load_stacks(net, sp, 1, qs[1], ks[1], stack[1])
                neg_rows(sp, 0)
                for g in range(2, NG):
                    neg_rows(sp, g - 1)
                    sp.wait_ge(S["scores"], steps * (g - 1))
                    load_stacks(net, sp, g, qs[g % 2], ks[g % 2], stack[g % 2])
                neg_rows(sp, NG - 1)
                sp.wait_ge(S["neg_landed"], 48 * NG)

            @block.tensor
            def _(pe):
                n = [0]

                def do_side(key):
                    for u in side.get(key, []):
                        i = n[0]
                        n[0] += 1
                        bank = bank_of(i)
                        depth = 4 if i < first else 2
                        if i >= depth:
                            pe.wait_ge(S["mx_used"], i - depth + 1)
                        if u[0] == "max":
                            _, g, h, t, k0, k1, _ = u
                            if h == 0 and t == 0:
                                pe.wait_ge(stack[g % 2], 96 * (g // 2 + 1))
                            lo, hi = keys_of(t)
                            last = nc.tensor.matmul(bank[:, 0:k1 - k0], qs[g % 2][0:R, h, t * P:(t + 1) * P],
                                                    ks[g % 2][0:R, h, k0:k1], start=True, stop=(mode == "full" or k1 < hi))
                            if mode == "causal" and k1 == hi:
                                last = nc.tensor.matmul(bank[:, hi - P - k0:hi - k0], net.ident_bf, net.later_qk,
                                                        start=False, stop=True)
                            if mode == "band":
                                at = 3 * P - (hi - lo)
                                for a, z in ((0, P + EDGE), (2 * P, 3 * P)):
                                    if z > at:
                                        a = max(a, at)
                                        last = nc.tensor.matmul(bank[:, a - at:z - at], net.ident_bf, net.band_qk[:, a:z],
                                                                start=False, stop=(z == 3 * P))
                            last.then_inc(S["mx_full"], 1)
                        elif u[0] == "turn_max":
                            pe.wait_ge(S["combined"], u[1] + 1)
                            nc.tensor.transpose(bank[0:GH * NT, 0:P], mrow[:, :], net.ident).then_inc(S["mx_full"], 1)
                        else:
                            pe.wait_ge(S["o_copied"], u[1] + 1)
                            for j in range(4):
                                t = 4 * u[2] + j
                                last = nc.tensor.transpose(bank[:, j * P:(j + 1) * P], osb[:, t * P:(t + 1) * P], net.ident)
                            last.then_inc(S["mx_full"], 1)

                def values(j):
                    g, i = divmod(j, steps)
                    for kt, q0, q1 in quarters[i]:
                        if kt == 0 and q0 == 0:
                            if g >= 1:
                                pe.wait_ge(S["o_copied"], g)
                            for bank in range(2):
                                for h in range(GH):
                                    nc.tensor.matmul(ps_o[32 * h:32 * h + 32, bank * HALF:(bank + 1) * HALF], net.zeros_bf[:, 0:32],
                                                     net.zeros_bf[:, :], start=True, stop=False)
                            pe.wait_ge(S["v_ready"], g + 1)
                        lo, hi = queries_of(kt)
                        if q0 == lo:
                            pe.wait_ge(S["exped"], GH * (g * NT + kt + 1))
                        bank = q0 // HALF
                        stop = kt == last_of[bank] and q1 == min(hi, (bank + 1) * HALF)
                        for h in range(GH):
                            last = nc.tensor.matmul(ps_o[32 * h:32 * h + 32, q0:q1], vst[:, g % 2, kt, h, :],
                                                    prob[:, kt % 2, h, q0:q1], start=False, stop=stop)
                        if q1 == hi:
                            last.then_inc(S["summed"], 1)

                do_side((-1, 0, 0))
                pe.wait_ge(S["mx_used"], first)
                for g in range(NG):
                    for i in range(steps):
                        kt, h = divmod(i, GH)
                        u = g * steps + i
                        if i == 0:
                            pe.wait_ge(S["neg_landed"], 48 * (g + 1))
                        if u >= 2:
                            pe.wait_ge(S["exped"], u - 1)
                        lo, hi = queries_of(kt)
                        pieces = split(lo, hi, HALF)
                        for q0, q1 in pieces:
                            if mode == "band":
                                masks = [(net.band_kq, max(a, q0 - lo), min(z, q1 - lo)) for a, z in ((0, P), (2 * P - EDGE, 3 * P))]
                            else:
                                masks = [(net.later_kq, 0, P)] if mode == "causal" and q0 == lo else []
                            masks = [(mask, a, z) for mask, a, z in masks if z > a]
                            last = nc.tensor.matmul(ps_st[:, u % 2, q0:q1], ks[g % 2][0:KR, h, kt * P:(kt + 1) * P],
                                                    qs[g % 2][0:KR, h, q0:q1], start=True, stop=not masks)
                            for n_mask, (mask, a, z) in enumerate(masks):
                                last = nc.tensor.matmul(ps_st[:, u % 2, lo + a:lo + z], net.ident_bf, mask[:, a:z],
                                                        start=False, stop=(n_mask == len(masks) - 1))
                        last.then_inc(S["scores"], 1)
                        do_side((g, i, 0))
                        if u >= GH + lag:
                            values(u - GH - lag)
                        do_side((g, i, 1))
                for j in range(NG * steps - GH - lag, NG * steps):
                    values(j)
                do_side((NG, 0, 0))

            @block.scalar
            def _(act):
                def take_output(g):
                    act.wait_ge(S["summed"], NT * (g + 1))
                    if g >= 1:
                        act.wait_ge(S["mx_used"], turned_before[g])
                    nc.scalar.activation(osb[:, :], ps_o[:, :], ACT.Copy).then_inc(S["o_copied"], 1)

                for g in range(NG):
                    for i in range(steps):
                        kt, h = divmod(i, GH)
                        u = g * steps + i
                        a = g * NT + kt
                        act.wait_ge(S["scores"], u + 1)
                        if h == 0 and a >= 2:
                            act.wait_ge(S["summed"], a - 1)
                        lo, hi = queries_of(kt)
                        nc.scalar.activation(prob[:, kt % 2, h, lo:hi], ps_st[:, u % 2, lo:hi], ACT.Exp,
                                             scale=scale).then_inc(S["exped"], 1)
                        if g > 0 and i == GH + lag - 1:
                            take_output(g - 1)
                take_output(NG - 1)

            @block.vector
            def _(dve):
                nc.vector.memset(ks[1][64:96, :, :].bitcast(U32), 0x3F803F80).then_inc(S["init"], 1)
                nc.vector.memset(mhalf[:, :, :], -3e38).then_inc(S["init"], 1)
                dve.wait_ge(S["init"], 2)
                i = 0
                small = 0
                for key in order:
                    for u in side.get(key, []):
                        if u[0] == "max":
                            _, g, h, t, k0, k1, half = u
                            dve.wait_ge(S["mx_full"], i + 1)
                            if h == 0 and t == 0 and g >= 1:
                                dve.wait_ge(S["combined"], g)
                            nc.vector.tensor_reduce(mhalf[:, h * NT + t, half:half + 1], bank_of(i)[:, 0:k1 - k0],
                                                    AX.X, ALU.max).then_inc(S["mx_used"], 1)
                        elif u[0] == "turn_max":
                            g = u[1]
                            dve.wait_ge(S["mx_used"], i)
                            nc.vector.tensor_reduce(mrow[:, :], mhalf[:, :, :], AX.X, ALU.max).then_inc(S["combined"], 1)
                            dve.wait_ge(S["mx_full"], i + 1)
                            m = mx[0:GH * NT, i % 2, 0:P]
                            if g >= 2:
                                dve.wait_ge(S["neg_landed"], 48 * (g - 1))
                            nc.vector.tensor_scalar(neg[:, g % 2, 0, :], m, -1.0, None, ALU.mult).then_inc(S["neg_step"], 1)
                            dve.wait_ge(S["neg_step"], small + 1)
                            nc.vector.scalar_tensor_tensor(out=nrest[:, :], in0=m, scalar=-1.0, in1=neg[:, g % 2, 0, :],
                                                           op0=ALU.mult, op1=ALU.subtract).then_inc(S["neg_step"], 1)
                            dve.wait_ge(S["neg_step"], small + 2)
                            nc.vector.tensor_copy(neg[:, g % 2, 1, :], nrest[:, :]).then_inc(S["neg_step"], 1)
                            dve.wait_ge(S["neg_step"], small + 3)
                            nc.vector.tensor_tensor(neg[:, g % 2, 2, :], nrest[:, :], neg[:, g % 2, 1, :],
                                                    ALU.subtract).then_inc(S["neg"], 1)
                            small += 3
                            dve.wait_ge(S["neg"], g + 1)
                            dve.sem_inc(S["mx_used"], 1)
                        else:
                            g, hf = u[1], u[2]
                            dve.wait_ge(S["mx_full"], i + 1)
                            dve.wait_ge(S["mx_used"], i)
                            o = mx[:, i % 2, :].rearrange("p (t h c) -> p t h c", t=4, h=GH)
                            nc.vector.reciprocal(rec[:, :, :], o[:, :, :, DH]).then_inc(S["recip"], 1)
                            dve.wait_ge(S["recip"], 2 * g + hf + 1)
                            dst = net.ctx_tok[:, 4 * hf:4 * hf + 4, g * GH * DH:(g + 1) * GH * DH].rearrange(
                                "p t (h d) -> p t h d", h=GH)
                            nc.vector.tensor_tensor(dst, o[:, :, :, 0:DH], rec[:, :, :].unsqueeze(3).broadcast_to([P, 4, GH, DH]),
                                                    ALU.mult).then_inc(S["mx_used"], 1)
                        i += 1

            @block.gpsimd
            def _(pool):
                nc.gpsimd.memset(vst[:, :, :, :, :], 0.0).then_inc(S["v_init"], 1)
                pool.wait_ge(S["v_init"], 1)
                nc.gpsimd.memset(vst[:, :, :, :, DH:DH + 1].rearrange("p b t h o -> p (b t h) o"), 1.0).then_inc(S["v_init"], 1)
                pool.wait_ge(S["v_init"], 2)
                for g in range(NG):
                    if g >= 2:
                        pool.wait_ge(S["summed"], NT * (g - 1))
                    nc.gpsimd.tensor_copy(vst[:, g % 2, :, :, 0:DH],
                                          net.v_tok[:, :, g * GH * DH:(g + 1) * GH * DH].rearrange(
                                              "p t (h d) -> p t h d", h=GH)).then_inc(S["v_ready"], 1)


def linear_tok(net, src_tok, w, dst_tok, bias=None, plus=None):
    nc = net.nc
    with net.phase("lin", ["turned", "ch", "product", "added"]) as (S, blk):
        turn = net.psum("turn", [P, 2, HALF])
        out = net.psum("out", [P, 2, HALF])
        ch = net.tmp("ch", [P, T])
        with blk as block:
            @block.sync
            def _(sp):
                net.clear_previous(sp)

            @block.tensor
            def _(pe):
                for i in range(2):
                    for j in range(4):
                        last = nc.tensor.transpose(turn[:, i, j * P:(j + 1) * P], src_tok[:, 4 * i + j, :], net.ident)
                    last.then_inc(S["turned"], 1)
                for i in range(2):
                    pe.wait_ge(S["ch"], i + 1)
                    for j in range(4):
                        t = 4 * i + j
                        last = nc.tensor.matmul(out[:, i, j * C:(j + 1) * C], ch[:, t * P:(t + 1) * P], w, start=True, stop=True)
                    last.then_inc(S["product"], 1)

            @block.scalar
            def _(act):
                for i in range(2):
                    act.wait_ge(S["turned"], i + 1)
                    nc.scalar.activation(ch[:, i * HALF:(i + 1) * HALF], turn[:, i, :], ACT.Copy).then_inc(S["ch"], 1)

            @block.vector
            def _(dve):
                for i in range(2):
                    dve.wait_ge(S["product"], i + 1)
                    d = dst_tok[:, 4 * i:4 * i + 4, :]
                    o = out[:, i, :].rearrange("p (t c) -> p t c", t=4)
                    if bias is None:
                        nc.vector.tensor_copy(d, o).then_inc(S["added"], 1)
                    else:
                        nc.vector.tensor_tensor(d, o, bias.unsqueeze(1).broadcast_to([P, 4, C]), ALU.add).then_inc(S["added"], 1)
                if plus is not None:
                    dve.wait_ge(S["added"], 2)
                    nc.vector.tensor_tensor(dst_tok[:, :, :], dst_tok[:, :, :], plus[:, :, :], ALU.add).then_inc(S["added"], 1)


def gate_update(net, g_tok):
    nc = net.nc
    with net.phase("gate", ["silu", "product", "sum"]) as (S, blk):
        act_g = net.tmp("act_g", [P, NT, C])
        with blk as block:
            @block.sync
            def _(sp):
                net.clear_previous(sp)

            @block.scalar
            def _(act):
                for i in range(2):
                    nc.scalar.activation(act_g[:, 4 * i:4 * i + 4, :], g_tok[:, 4 * i:4 * i + 4, :], ACT.Silu).then_inc(S["silu"], 1)

            @block.vector
            def _(dve):
                for i in range(2):
                    ts = slice(4 * i, 4 * i + 4)
                    dve.wait_ge(S["silu"], i + 1)
                    nc.vector.tensor_tensor(act_g[:, ts, :], act_g[:, ts, :], net.s_tok[:, ts, :], ALU.mult).then_inc(S["product"], 1)
                    dve.wait_ge(S["product"], i + 1)
                    nc.vector.tensor_tensor(net.x_tok[:, ts, :], net.x_tok[:, ts, :], act_g[:, ts, :], ALU.add).then_inc(S["sum"], 1)


def rwkv_ffn(net, out_tok):
    nc, W = net.nc, net.W
    with net.phase("rwkv", ["prev", "diff", "mix_k", "mix_r", "mm_k", "relu", "square", "mm_r", "sig", "mm_v", "out"]) as (S, blk):
        prev = net.tmp("prev", [P, T + 1])
        diff = net.tmp("diff", [P, T])
        xk = net.tmp("xk", [P, T])
        xr = net.tmp("xr", [P, T])
        ka = net.tmp("ka", [P, T])
        r_tok = net.tmp("r_tok", [P, 2, HALF])
        pk = net.psum("pk", [P, 2, HALF])
        pr = net.psum("pr", [P, 2, HALF])
        pv = net.psum("pv", [P, 2, HALF])
        with blk as block:
            @block.sync
            def _(sp):
                net.clear_previous(sp)
                store_keys(net, sp)
                load_first_stacks(net, sp)

            @block.gpsimd
            def _(pool):
                nc.gpsimd.memset(prev[:, 0:1], 0.0).then_inc(S["prev"], 1)

            @block.vector
            def _(dve):
                nc.vector.tensor_copy(prev[:, 1:T + 1], net.xn_ch[:, :]).then_inc(S["prev"], 1)
                dve.wait_ge(S["prev"], 2)
                nc.vector.tensor_tensor(diff[:, :], net.xn_ch[:, :], prev[:, 0:T], ALU.subtract).then_inc(S["diff"], 1)
                dve.wait_ge(S["diff"], 1)
                for i in range(2):
                    cs = slice(i * HALF, (i + 1) * HALF)
                    nc.vector.scalar_tensor_tensor(out=xk[:, cs], in0=diff[:, cs], scalar=W("l0_mu_k"), in1=prev[:, cs],
                                                   op0=ALU.mult, op1=ALU.add).then_inc(S["mix_k"], 1)
                for i in range(2):
                    cs = slice(i * HALF, (i + 1) * HALF)
                    nc.vector.scalar_tensor_tensor(out=xr[:, cs], in0=diff[:, cs], scalar=W("l0_mu_r"), in1=prev[:, cs],
                                                   op0=ALU.mult, op1=ALU.add).then_inc(S["mix_r"], 1)
                for i in range(2):
                    cs = slice(i * HALF, (i + 1) * HALF)
                    dve.wait_ge(S["relu"], i + 1)
                    nc.vector.tensor_tensor(ka[:, cs], ka[:, cs], ka[:, cs], ALU.mult).then_inc(S["square"], 1)
                for i in range(2):
                    dve.wait_ge(S["mm_v"], i + 1)
                    dve.wait_ge(S["sig"], i + 1)
                    nc.vector.tensor_tensor(out_tok[:, 4 * i:4 * i + 4, :], pv[:, i, :].rearrange("p (t c) -> p t c", t=4),
                                            r_tok[:, i, :].rearrange("p (t c) -> p t c", t=4), ALU.mult).then_inc(S["out"], 1)

            @block.scalar
            def _(act):
                for i in range(2):
                    act.wait_ge(S["mm_k"], i + 1)
                    nc.scalar.activation(ka[:, i * HALF:(i + 1) * HALF], pk[:, i, :], ACT.Relu).then_inc(S["relu"], 1)
                for i in range(2):
                    act.wait_ge(S["mm_r"], i + 1)
                    nc.scalar.activation(r_tok[:, i, :], pr[:, i, :], ACT.Sigmoid).then_inc(S["sig"], 1)

            @block.tensor
            def _(pe):
                for i in range(2):
                    pe.wait_ge(S["mix_k"], i + 1)
                    nc.tensor.matmul(pk[:, i, :], W("l0_k"), xk[:, i * HALF:(i + 1) * HALF], start=True, stop=True).then_inc(S["mm_k"], 1)
                for i in range(2):
                    pe.wait_ge(S["mix_r"], i + 1)
                    for j in range(4):
                        t = 4 * i + j
                        last = nc.tensor.matmul(pr[:, i, j * C:(j + 1) * C], xr[:, t * P:(t + 1) * P], W("l0_r"), start=True, stop=True)
                    last.then_inc(S["mm_r"], 1)
                for i in range(2):
                    pe.wait_ge(S["square"], i + 1)
                    for j in range(4):
                        t = 4 * i + j
                        last = nc.tensor.matmul(pv[:, i, j * C:(j + 1) * C], ka[:, t * P:(t + 1) * P], W("l0_v"), start=True, stop=True)
                    last.then_inc(S["mm_v"], 1)


def route(net, gate_w, gate_b, temp):
    nc = net.nc
    E = 8
    with net.phase("route", ["logits", "step", "exp", "top", "idx"]) as (S, blk):
        lg = net.tmp("lg", [P, NT, E])
        red = net.tmp("red", [P, NT])
        inv = net.tmp("inv", [P, NT])
        ti = net.tmp("ti", [P, NT, E], U32)
        ps = net.psum("ps", [P, NT, E])
        with blk as block:
            @block.sync
            def _(sp):
                net.clear_previous(sp)
                store_keys(net, sp)

            @block.tensor
            def _(pe):
                for t in range(NT):
                    last = nc.tensor.matmul(ps[:, t, :], net.xn_ch[:, t * P:(t + 1) * P], gate_w, start=True, stop=True)
                last.then_inc(S["logits"], 1)

            @block.scalar
            def _(act):
                act.wait_ge(S["step"], 3)
                nc.scalar.activation(lg[:, :, :], lg[:, :, :], ACT.Exp, scale=1.0 / temp).then_inc(S["exp"], 1)

            @block.vector
            def _(dve):
                per_tile = lambda a: a[:, :].unsqueeze(2).broadcast_to([P, NT, E])
                dve.wait_ge(S["logits"], 1)
                nc.vector.tensor_tensor(lg[:, :, :], ps[:, :, :], gate_b.unsqueeze(1).broadcast_to([P, NT, E]), ALU.add).then_inc(S["step"], 1)
                dve.wait_ge(S["step"], 1)
                nc.vector.tensor_reduce(red[:, :], lg[:, :, :], AX.X, ALU.max).then_inc(S["step"], 1)
                dve.wait_ge(S["step"], 2)
                nc.vector.tensor_tensor(lg[:, :, :], lg[:, :, :], per_tile(red), ALU.subtract).then_inc(S["step"], 1)
                dve.wait_ge(S["exp"], 1)
                nc.vector.tensor_reduce(inv[:, :], lg[:, :, :], AX.X, ALU.add).then_inc(S["step"], 1)
                dve.wait_ge(S["step"], 4)
                nc.vector.reciprocal(red[:, :], inv[:, :]).then_inc(S["step"], 1)
                dve.wait_ge(S["step"], 5)
                nc.vector.tensor_tensor(lg[:, :, :], lg[:, :, :], per_tile(red), ALU.mult).then_inc(S["step"], 1)
                dve.wait_ge(S["step"], 6)
                for t in range(NT):
                    nc.vector.max(net.top[:, t, :], lg[:, t, :]).then_inc(S["top"], 1)
                for t in range(NT):
                    dve.wait_ge(S["top"], t + 1)
                    nc.vector.max_index(ti[:, t, :], net.top[:, t, :], lg[:, t, :]).then_inc(S["idx"], 1)
                dve.wait_ge(S["idx"], NT)
                nc.vector.tensor_copy(net.top_i[:, :, :], ti[:, :, :]).then_inc(S["step"], 1)


def moe(net, out_tok):
    nc, W = net.nc, net.W
    E, HB = 8, 2
    route(net, W("l1_wg"), W("l1_bg"), 5.0)
    units = [(e, c) for e in range(E) for c in range(2)]
    with net.phase("moe", ["step", "gate", "gate_t", "gt", "base", "acc", "hid", "gelu", "outp", "taken"]) as (S, blk):
        den = net.tmp("den", [P, NT])
        v = net.tmp("v", [P, NT, 2])
        g0 = net.tmp("g0", [P, NT, E])
        g1 = net.tmp("g1", [P, NT, E])
        gate = net.tmp("gate", [P, NT, E])
        gate_t = net.tmp("gate_t", [E, T])
        h = net.tmp("h", [P, 2, HB, HALF])
        ph = net.psum("ph", [P, 2, HB, HALF])
        po = net.psum("po", [P, 2, HALF])
        pg = net.psum("pg", [P, 2, HALF])
        with blk as block:
            @block.sync
            def _(sp):
                net.clear_previous(sp)
                load_first_stacks(net, sp)

            @block.vector
            def _(dve):
                n = [0]

                def step(ins):
                    n[0] += 1
                    ins.then_inc(S["step"], 1)
                    dve.wait_ge(S["step"], n[0])

                iota = net.K("iota8").unsqueeze(1).broadcast_to([P, NT, E])
                per = lambda a: a.broadcast_to([P, NT, E])
                step(nc.vector.tensor_tensor(den[:, :], net.top[:, :, 0], net.top[:, :, 1], ALU.add))
                step(nc.vector.tensor_scalar(den[:, :], den[:, :], 1e-9, None, ALU.add))
                step(nc.vector.reciprocal(v[:, :, 0], den[:, :]))
                step(nc.vector.tensor_tensor(v[:, :, 1], net.top[:, :, 1], v[:, :, 0], ALU.mult))
                step(nc.vector.tensor_tensor(v[:, :, 0], net.top[:, :, 0], v[:, :, 0], ALU.mult))
                step(nc.vector.tensor_tensor(g0[:, :, :], iota, per(net.top_i[:, :, 0:1]), ALU.is_equal))
                step(nc.vector.tensor_tensor(g1[:, :, :], iota, per(net.top_i[:, :, 1:2]), ALU.is_equal))
                step(nc.vector.tensor_tensor(g0[:, :, :], g0[:, :, :], per(v[:, :, 0:1]), ALU.mult))
                step(nc.vector.tensor_tensor(g1[:, :, :], g1[:, :, :], per(v[:, :, 1:2]), ALU.mult))
                nc.vector.tensor_tensor(gate[:, :, :], g0[:, :, :], g1[:, :, :], ALU.add).then_inc(S["gate"], 1)
                dve.wait_ge(S["gate_t"], 1)
                nc.vector.tensor_copy(gate_t[:, :], pg[0:E, :, :].rearrange("p a b -> p (a b)")).then_inc(S["gt"], 1)
                for i in range(2):
                    dve.wait_ge(S["base"], i + 1)
                    nc.vector.tensor_copy(out_tok[:, 4 * i:4 * i + 4, :], pg[:, i, :].rearrange("p (t c) -> p t c", t=4)).then_inc(S["acc"], 1)
                for u, (e, c) in enumerate(units):
                    dve.wait_ge(S["outp"], u + 1)
                    dve.wait_ge(S["acc"], 2 if e == 0 else 2 + 4 * (u - 1))
                    for j in range(4):
                        t = 4 * c + j
                        last = nc.vector.scalar_tensor_tensor(out=out_tok[:, t, :], in0=po[:, u % 2, j * C:(j + 1) * C],
                                                              scalar=gate[:, t, e:e + 1], in1=out_tok[:, t, :],
                                                              op0=ALU.mult, op1=ALU.add).then_inc(S["acc"], 1)

            @block.scalar
            def _(act):
                for u, (e, c) in enumerate(units):
                    act.wait_ge(S["hid"], u + 1)
                    if u >= 2:
                        act.wait_ge(S["outp"], u - 1)
                    for j in range(HB):
                        last = nc.scalar.activation(h[:, u % 2, j, :], ph[:, u % 2, j, :], ACT.Gelu,
                                                    bias=W(f"l1_b1_{e}", HB, j))
                    last.then_inc(S["gelu"], 1)

            @block.tensor
            def _(pe):
                def hidden(u):
                    e, c = units[u]
                    if u >= 2:
                        pe.wait_ge(S["gelu"], u - 1)
                    for j in range(HB):
                        last = nc.tensor.matmul(ph[:, u % 2, j, :], W(f"l1_w1_{e}")[:, j * P:(j + 1) * P],
                                                net.xn_ch[:, c * HALF:(c + 1) * HALF], start=True, stop=True)
                    last.then_inc(S["hid"], 1)

                hidden(0)
                hidden(1)
                pe.wait_ge(S["gate"], 1)
                for t in range(NT):
                    last = nc.tensor.transpose(pg[0:E, t // 4, t % 4 * P:(t % 4 + 1) * P], gate[:, t, :], net.ident)
                last.then_inc(S["gate_t"], 1)
                pe.wait_ge(S["gt"], 1)
                for t in range(NT):
                    last = nc.tensor.matmul(pg[:, t // 4, t % 4 * C:(t % 4 + 1) * C], gate_t[:, t * P:(t + 1) * P], W("l1_b2"),
                                            start=True, stop=True)
                    if t % 4 == 3:
                        last.then_inc(S["base"], 1)
                for u, (e, c) in enumerate(units):
                    pe.wait_ge(S["gelu"], u + 1)
                    if u >= 2:
                        pe.wait_ge(S["acc"], 2 + 4 * (u - 1))
                    for t in range(4):
                        for j in range(HB):
                            last = nc.tensor.matmul(po[:, u % 2, t * C:(t + 1) * C], h[:, u % 2, j, t * P:(t + 1) * P],
                                                    W(f"l1_w2_{e}", HB, j), start=(j == 0), stop=(j == HB - 1))
                    last.then_inc(S["outp"], 1)
                    if u + 2 < len(units):
                        hidden(u + 2)


def relu_ffn(net):
    nc, W = net.nc, net.W
    FB = 4
    units = [(c, j) for c in range(2) for j in range(FB)]
    with net.phase("relu_ffn", ["hid", "act", "outp", "biased", "sum"]) as (S, blk):
        h = net.tmp("h", [P, FB, T])
        ph = net.psum("ph", [P, 4, HALF])
        po = net.psum("po", [P, 2, HALF])
        with blk as block:
            @block.sync
            def _(sp):
                net.clear_previous(sp)

            @block.tensor
            def _(pe):
                for u, (c, j) in enumerate(units):
                    if u >= 4:
                        pe.wait_ge(S["act"], u - 3)
                    nc.tensor.matmul(ph[:, u % 4, :], W("l2_w1")[:, j * P:(j + 1) * P], net.in_ch[:, c * HALF:(c + 1) * HALF],
                                     start=True, stop=True).then_inc(S["hid"], 1)
                for c in range(2):
                    pe.wait_ge(S["act"], FB * (c + 1))
                    for t in range(4 * c, 4 * c + 4):
                        for j in range(FB):
                            last = nc.tensor.matmul(po[:, c, t % 4 * C:(t % 4 + 1) * C], h[:, j, t * P:(t + 1) * P],
                                                    W("l2_w2", FB, j), start=(j == 0), stop=(j == FB - 1))
                    last.then_inc(S["outp"], 1)

            @block.scalar
            def _(act):
                for u, (c, j) in enumerate(units):
                    act.wait_ge(S["hid"], u + 1)
                    nc.scalar.activation(h[:, j, c * HALF:(c + 1) * HALF], ph[:, u % 4, :], ACT.Relu,
                                         bias=W("l2_b1", FB, j)).then_inc(S["act"], 1)

            @block.vector
            def _(dve):
                nc.vector.tensor_tensor(net.s_tok[:, :, :], net.s_tok[:, :, :], W("l2_b2").unsqueeze(1).broadcast_to([P, NT, C]),
                                        ALU.add).then_inc(S["biased"], 1)
                dve.wait_ge(S["biased"], 1)
                for c in range(2):
                    ts = slice(4 * c, 4 * c + 4)
                    dve.wait_ge(S["outp"], c + 1)
                    nc.vector.tensor_tensor(net.s_tok[:, ts, :], po[:, c, :].rearrange("p (t c) -> p t c", t=4),
                                            net.s_tok[:, ts, :], ALU.add).then_inc(S["sum"], 1)


def switch_ffn(net, out_tok):
    nc, W = net.nc, net.W
    E, CAP, FB = 8, 80, 4
    SL = E * CAP
    o_w1, o_w2, o_b2 = (net.stream_where[n][0] for n in ("w1", "w2", "b2"))
    route(net, W("l2_gw"), W("l2_gb"), 1.0)
    with net.phase("switch", ["landed", "step", "mask", "cum", "slot", "sec", "disp", "disp_sb", "hid", "gelu", "outp", "eo",
                              "slot_bc", "bc_sb", "sec_t", "comb", "done"]) as (S, blk):
        wst = net.tmp("wst", [P, net.streams.shape[1]])
        mask = net.tmp("mask", [P, NT, E])
        base = net.tmp("base", [P, NT + 1, E])
        cum = net.tmp("cum", [P, NT, E])
        pos = net.tmp("pos", [P, NT])
        keep = net.tmp("keep", [P, NT])
        slot = net.tmp("slot", [P, NT])
        sec = net.tmp("sec", [P, 2, SL])
        disp = net.s_tok[:, 0:SL // C, :].rearrange("p t c -> p (t c)")
        h = net.tmp("h", [P, 2, FB * CAP])
        eo = net.ctx_tok[0:CAP, :, :]
        bcs = net.in_ch[0:CAP, :]
        sec_t = net.tmp("sec_t", [CAP, 2, E, P])
        pc = net.psum("pc", [P, HALF])
        pd = net.psum("pd", [P, 2, HALF])
        ph = net.psum("ph", [P, 2, HALF])
        pb = net.psum("pb", [P, 2, HALF])
        tot = NT * E

        def take(dve, t):
            dve.wait_ge(S["comb"], t + 1)
            nc.vector.tensor_scalar(out_tok[:, t, :], pd[:, t % 2, 0:C], net.top[:, t, 0:1], None, ALU.mult).then_inc(S["done"], 1)

        with blk as block:
            @block.sync
            def _(sp):
                net.clear_previous(sp)
                sp.dma_start(wst[:, :], net.streams).then_inc(S["landed"], 16)
                load_first_stacks(net, sp)

            @block.vector
            def _(dve):
                n = [0]

                def step(ins):
                    n[0] += 1
                    ins.then_inc(S["step"], 1)
                    dve.wait_ge(S["step"], n[0])

                nc.vector.tensor_tensor(mask[:, :, :], net.K("iota8").unsqueeze(1).broadcast_to([P, NT, E]),
                                        net.top_i[:, :, 0:1].broadcast_to([P, NT, E]), ALU.is_equal).then_inc(S["mask"], 1)
                dve.wait_ge(S["mask"], 1)
                step(nc.vector.tensor_copy(base[:, 0, :], net.count[:, :]))
                dve.wait_ge(S["cum"], 1)
                for t in range(NT):
                    step(nc.vector.tensor_tensor(base[:, t + 1, :], base[:, t, :], pc[:, tot + t * E:tot + (t + 1) * E], ALU.add))
                step(nc.vector.tensor_copy(net.count[:, :], base[:, NT, :]))
                step(nc.vector.tensor_tensor(cum[:, :, :], pc[:, 0:tot].rearrange("p (t e) -> p t e", t=NT), base[:, 0:NT, :], ALU.add))
                step(nc.vector.tensor_tensor(cum[:, :, :], cum[:, :, :], mask[:, :, :], ALU.mult))
                step(nc.vector.tensor_reduce(pos[:, :], cum[:, :, :], AX.X, ALU.add))
                step(nc.vector.tensor_scalar(keep[:, :], pos[:, :], float(CAP), None, ALU.is_le))
                step(nc.vector.scalar_tensor_tensor(out=slot[:, :], in0=net.top_i[:, :, 0], scalar=float(CAP), in1=pos[:, :],
                                                    op0=ALU.mult, op1=ALU.add))
                step(nc.vector.tensor_tensor(slot[:, :], slot[:, :], keep[:, :], ALU.mult))
                nc.vector.tensor_scalar(slot[:, :], slot[:, :], -1.0, None, ALU.add).then_inc(S["slot"], 1)
                dve.wait_ge(S["slot"], 1)
                for t in range(NT):
                    if t >= 2:
                        dve.wait_ge(S["disp"], t - 1)
                    nc.vector.tensor_scalar(sec[:, t % 2, :], net.K("iota640"), slot[:, t:t + 1], None,
                                            ALU.is_equal).then_inc(S["sec"], 1)
                dve.wait_ge(S["disp"], NT)
                for i in range(2):
                    nc.vector.tensor_copy(disp[:, i * SL // 2:(i + 1) * SL // 2], pd[:, i, 0:SL // 2]).then_inc(S["disp_sb"], 1)
                for i in range(2):
                    dve.wait_ge(S["slot_bc"], i + 1)
                    nc.vector.tensor_copy(bcs[:, i * HALF:(i + 1) * HALF], pb[0:CAP, i, :]).then_inc(S["bc_sb"], 1)
                for e in range(E):
                    dve.wait_ge(S["outp"], e + 1)
                    nc.vector.tensor_tensor(eo[:, e, :], pb[0:CAP, e % 2, 0:C], wst[0:CAP, o_b2 + e * C:o_b2 + (e + 1) * C],
                                            ALU.add).then_inc(S["eo"], 1)
                dve.wait_ge(S["bc_sb"], 2)
                for t in range(NT):
                    if t >= 2:
                        dve.wait_ge(S["comb"], t - 1)
                    nc.vector.tensor_tensor(sec_t[:, t % 2, :, :], bcs[:, t * P:(t + 1) * P].unsqueeze(1).broadcast_to([CAP, E, P]),
                                            net.K("slot_id")[0:CAP, :].unsqueeze(2).broadcast_to([CAP, E, P]), ALU.is_equal).then_inc(S["sec_t"], 1)
                    if t >= 1:
                        take(dve, t - 1)
                take(dve, NT - 1)

            @block.scalar
            def _(act):
                for e in range(E):
                    act.wait_ge(S["hid"], e + 1)
                    if e >= 2:
                        act.wait_ge(S["outp"], e - 1)
                    for j in range(FB):
                        last = nc.scalar.activation(h[:, e % 2, j * CAP:(j + 1) * CAP], ph[:, e % 2, j * CAP:(j + 1) * CAP],
                                                    ACT.Gelu_apprx_tanh, bias=W("l2_eb1", E * FB, e * FB + j))
                    last.then_inc(S["gelu"], 1)

            @block.tensor
            def _(pe):
                pe.wait_ge(S["mask"], 1)
                masks = mask[:, :, :].rearrange("p t e -> p (t e)")
                nc.tensor.matmul(pc[:, 0:tot], net.K("tri"), masks, start=True, stop=True)
                nc.tensor.matmul(pc[:, tot:2 * tot], net.K("ones"), masks, start=True, stop=True).then_inc(S["cum"], 1)
                for t in range(NT):
                    pe.wait_ge(S["sec"], t + 1)
                    for i in range(2):
                        last = nc.tensor.matmul(pd[:, i, 0:SL // 2], net.xn_tok[:, t, :], sec[:, t % 2, i * SL // 2:(i + 1) * SL // 2],
                                                start=(t == 0), stop=(t == NT - 1))
                    last.then_inc(S["disp"], 1)
                for t in range(NT):
                    last = nc.tensor.matmul(pb[:, t // 4, t % 4 * P:(t % 4 + 1) * P], slot[:, t:t + 1].broadcast_to([P, P]),
                                            net.ident, start=True, stop=True)
                    if t % 4 == 3:
                        last.then_inc(S["slot_bc"], 1)
                pe.wait_ge(S["disp_sb"], 2)
                pe.wait_ge(S["bc_sb"], 2)
                pe.wait_ge(S["landed"], 16)

                def hidden(e):
                    if e >= 2:
                        pe.wait_ge(S["gelu"], e - 1)
                    for j in range(FB):
                        last = nc.tensor.matmul(ph[:, e % 2, j * CAP:(j + 1) * CAP],
                                                wst[:, o_w1 + (e * FB + j) * P:o_w1 + (e * FB + j + 1) * P],
                                                disp[:, e * CAP:(e + 1) * CAP], start=True, stop=True)
                    last.then_inc(S["hid"], 1)

                hidden(0)
                for e in range(E):
                    if e + 1 < E:
                        hidden(e + 1)
                    pe.wait_ge(S["gelu"], e + 1)
                    if e >= 2:
                        pe.wait_ge(S["eo"], e - 1)
                    for j in range(FB):
                        last = nc.tensor.matmul(pb[0:CAP, e % 2, 0:C], h[:, e % 2, j * CAP:(j + 1) * CAP],
                                                wst[:, o_w2 + (e * FB + j) * C:o_w2 + (e * FB + j + 1) * C],
                                                start=(j == 0), stop=(j == FB - 1))
                    last.then_inc(S["outp"], 1)
                pe.wait_ge(S["eo"], E)
                for t in range(NT):
                    pe.wait_ge(S["sec_t"], t + 1)
                    if t >= 2:
                        pe.wait_ge(S["done"], t - 1)
                    for e in range(E):
                        last = nc.tensor.matmul(pd[:, t % 2, 0:C], sec_t[:, t % 2, e, :], eo[:, e, :], start=(e == 0), stop=(e == E - 1))
                    last.then_inc(S["comb"], 1)


def mamba(net):
    nc, W = net.nc, net.W
    H, D, N = 4, 64, 64
    DI = H * D
    blocks = [(0, 128), (128, 128), (256, N), (320, N)]
    with ExitStack() as keep:
        def kept(name, shape):
            return keep.enter_context(nc.sbuf_tensor(name, shape, F32))
        x_tok = kept("m_x", [P, NT, DI])
        b_tok = kept("m_b", [P, NT, N])
        b_ch = kept("m_bch", [N, T])
        c_ch = kept("m_cch", [N, T])
        z_tok = kept("m_z", [P, NT, DI])
        y_tok = kept("m_y", [P, NT, DI])
        dt = kept("m_dt", [P, NT, H])
        da = kept("m_da", [P, NT, H])

        with net.phase("m_proj", ["zero", "pre", "padded", "conv", "silu", "turned", "tok", "zmm", "z", "dtmm", "step", "exp", "ln", "nega"]) as (S, blk):
            xp = net.tmp("xp", [P, 2, T + 3])
            acc = net.tmp("acc", [P, 2, T])
            xs = net.tmp("xs", [P, 2, T])
            u = net.tmp("u", [P, NT, H])
            e = net.tmp("e", [P, NT, H])
            v = net.tmp("v", [P, NT, H])
            na = net.tmp("na", [P, H])
            pp = net.psum("pp", [P, 2, HALF])
            pt = net.psum("pt", [P, 2, HALF])
            pz = net.psum("pz", [P, 2, HALF])
            pdt = net.psum("pdt", [P, NT, H])
            dest = [xs[:, 0, :], xs[:, 1, :], b_ch[:, :], c_ch[:, :]]
            turns = [(j, i) for j in range(3) for i in range(2)]

            def silu(act, j):
                m = blocks[j][1]
                act.wait_ge(S["conv"], 4 * (j + 1))
                nc.scalar.activation(dest[j], acc[0:m, j % 2, :], ACT.Silu).then_inc(S["silu"], 1)

            def to_tok(dve, j):
                m = blocks[j][1]
                for i in range(2):
                    k = 2 * j + i
                    dve.wait_ge(S["turned"], k + 1)
                    dst = b_tok[:, 4 * i:4 * i + 4, :] if j == 2 else x_tok[:, 4 * i:4 * i + 4, j * P:(j + 1) * P]
                    nc.vector.tensor_copy(dst, pt[:, k % 2, 0:4 * m].rearrange("p (t c) -> p t c", t=4)).then_inc(S["tok"], 1)

            with blk as block:
                @block.sync
                def _(sp):
                    net.clear_previous(sp)

                @block.gpsimd
                def _(pool):
                    nc.gpsimd.memset(xp[:, :, 0:3], 0.0).then_inc(S["zero"], 1)

                @block.tensor
                def _(pe):
                    def pre(j):
                        c0, m = blocks[j]
                        for i in range(2):
                            k = 2 * j + i
                            if k >= 2:
                                pe.wait_ge(S["padded"], k - 1)
                            nc.tensor.matmul(pp[0:m, k % 2, :], W("l3_xbc")[:, c0:c0 + m], net.in_ch[:, i * HALF:(i + 1) * HALF],
                                             start=True, stop=True).then_inc(S["pre"], 1)

                    for t in range(NT):
                        last = nc.tensor.matmul(pdt[:, t, :], net.in_ch[:, t * P:(t + 1) * P], W("l3_dt"), start=True, stop=True)
                    last.then_inc(S["dtmm"], 1)
                    for j in range(4):
                        pre(j)
                        for t in (2 * j, 2 * j + 1):
                            if t >= 4:
                                pe.wait_ge(S["z"], t - 3 - (t % 2))
                            last = nc.tensor.matmul(pz[:, t // 2 % 2, t % 2 * DI:(t % 2 + 1) * DI], net.in_ch[:, t * P:(t + 1) * P],
                                                    W("l3_z"), start=True, stop=True)
                            last.then_inc(S["zmm"], 1)
                    for k, (j, i) in enumerate(turns):
                        m = blocks[j][1]
                        pe.wait_ge(S["silu"], j + 1)
                        if k >= 2:
                            pe.wait_ge(S["tok"], k - 1)
                        for q in range(4):
                            last = nc.tensor.transpose(pt[:, k % 2, q * m:(q + 1) * m], dest[j][:, (4 * i + q) * P:(4 * i + q + 1) * P],
                                                       net.ident[0:m, 0:m])
                        last.then_inc(S["turned"], 1)

                @block.scalar
                def _(act):
                    act.wait_ge(S["step"], 2)
                    nc.scalar.activation(e[:, :, :], e[:, :, :], ACT.Exp, scale=-1.0).then_inc(S["exp"], 1)
                    nc.scalar.activation(na[:, :], W("l3_alog"), ACT.Exp).then_inc(S["nega"], 1)
                    act.wait_ge(S["step"], 3)
                    nc.scalar.activation(dt[:, :, :], v[:, :, :], ACT.Ln).then_inc(S["ln"], 1)
                    act.wait_ge(S["zero"], 1)
                    for j, (c0, m) in enumerate(blocks):
                        if j >= 2:
                            act.wait_ge(S["conv"], 4 * (j - 1))
                        for i in range(2):
                            act.wait_ge(S["pre"], 2 * j + i + 1)
                            nc.scalar.activation(xp[0:m, j % 2, 3 + i * HALF:3 + (i + 1) * HALF], pp[0:m, (2 * j + i) % 2, :],
                                                 ACT.Copy).then_inc(S["padded"], 1)
                        for t in (2 * j, 2 * j + 1):
                            act.wait_ge(S["zmm"], 2 * (t // 2) + 2)
                            nc.scalar.activation(z_tok[:, t, :], pz[:, t // 2 % 2, t % 2 * DI:(t % 2 + 1) * DI], ACT.Silu).then_inc(S["z"], 1)
                        if j >= 1:
                            silu(act, j - 1)
                    silu(act, 3)

                @block.vector
                def _(dve):
                    dve.wait_ge(S["dtmm"], 1)
                    nc.vector.tensor_tensor(u[:, :, :], pdt[:, :, :], W("l3_dtb").unsqueeze(1).broadcast_to([P, NT, H]), ALU.add).then_inc(S["step"], 1)
                    dve.wait_ge(S["step"], 1)
                    nc.vector.scalar_tensor_tensor(out=e[:, :, :], in0=u[:, :, :], scalar=-1.0, in1=u[:, :, :], op0=ALU.mult, op1=ALU.max).then_inc(S["step"], 1)
                    dve.wait_ge(S["exp"], 1)
                    nc.vector.tensor_scalar(v[:, :, :], e[:, :, :], 1.0, None, ALU.add).then_inc(S["step"], 1)
                    dve.wait_ge(S["step"], 3)
                    n = [3]

                    def step(ins):
                        n[0] += 1
                        ins.then_inc(S["step"], 1)
                        dve.wait_ge(S["step"], n[0])

                    step(nc.vector.scalar_tensor_tensor(out=da[:, :, :], in0=v[:, :, :], scalar=-1.0, in1=e[:, :, :],
                                                        op0=ALU.add, op1=ALU.subtract))
                    dve.wait_ge(S["ln"], 1)
                    step(nc.vector.reciprocal(v[:, :, :], v[:, :, :]))
                    step(nc.vector.tensor_tensor(da[:, :, :], da[:, :, :], v[:, :, :], ALU.mult))
                    step(nc.vector.tensor_tensor(dt[:, :, :], dt[:, :, :], da[:, :, :], ALU.subtract))
                    step(nc.vector.scalar_tensor_tensor(out=dt[:, :, :], in0=u[:, :, :], scalar=0.0, in1=dt[:, :, :],
                                                        op0=ALU.max, op1=ALU.add))
                    dve.wait_ge(S["nega"], 1)
                    step(nc.vector.scalar_tensor_tensor(out=da[:, :, :], in0=dt[:, :, :], scalar=-1.0,
                                                        in1=na[:, :].unsqueeze(1).broadcast_to([P, NT, H]), op0=ALU.mult, op1=ALU.mult))
                    for j, (c0, m) in enumerate(blocks):
                        dve.wait_ge(S["padded"], 2 * j + 2)
                        if j >= 2:
                            dve.wait_ge(S["silu"], j - 1)
                        src, dst = xp[0:m, j % 2, :], acc[0:m, j % 2, :]
                        cw = W(f"l3_cw{j}")
                        nc.vector.tensor_scalar(dst, src[:, 0:T], cw[:, 0:1], W(f"l3_cb{j}"), ALU.mult, ALU.add).then_inc(S["conv"], 1)
                        for k in range(1, 4):
                            dve.wait_ge(S["conv"], 4 * j + k)
                            nc.vector.scalar_tensor_tensor(out=dst, in0=src[:, k:k + T], scalar=cw[:, k:k + 1], in1=dst,
                                                           op0=ALU.mult, op1=ALU.add).then_inc(S["conv"], 1)
                        if j >= 1:
                            to_tok(dve, j - 1)

        with net.phase("m_decay", ["cums", "step", "exp", "state0"]) as (S, blk):
            cum = kept("m_cum", [P, NT, H])
            ecum = kept("m_ecum", [P, NT, H])
            etot = kept("m_etot", [P, NT, H])
            wend = kept("m_wend", [P, NT, H])
            xdt = kept("m_xdt", [P, NT, DI])
            xw = kept("m_xw", [P, NT, DI])
            state = kept("m_state", [N, 2, DI])
            ss = kept("m_ss", [P, NT])
            pcum = net.psum("pcum", [P, HALF])
            with blk as block:
                @block.sync
                def _(sp):
                    net.clear_previous(sp)

                @block.tensor
                def _(pe):
                    flat = da[:, :, :].rearrange("p t h -> p (t h)")
                    nc.tensor.matmul(pcum[:, 0:NT * H], net.K("tri"), flat, start=True, stop=True)
                    nc.tensor.matmul(pcum[:, NT * H:2 * NT * H], net.K("ones"), flat, start=True, stop=True).then_inc(S["cums"], 1)

                @block.vector
                def _(dve):
                    p_cum = pcum[:, 0:NT * H].rearrange("p (t h) -> p t h", h=H)
                    p_tot = pcum[:, NT * H:2 * NT * H].rearrange("p (t h) -> p t h", h=H)
                    wide = lambda a: a[:, :, :].rearrange("p t h -> p (t h)").unsqueeze(2).broadcast_to([P, NT * H, D])
                    heads = lambda a: a[:, :, :].rearrange("p t (h d) -> p (t h) d", h=H)
                    dve.wait_ge(S["cums"], 1)
                    nc.vector.tensor_copy(cum[:, :, :], p_cum).then_inc(S["step"], 1)
                    nc.vector.tensor_copy(etot[:, :, :], p_tot).then_inc(S["step"], 1)
                    dve.wait_ge(S["step"], 2)
                    nc.vector.tensor_tensor(wend[:, :, :], etot[:, :, :], cum[:, :, :], ALU.subtract).then_inc(S["step"], 1)
                    nc.vector.tensor_tensor(heads(xdt), heads(x_tok), wide(dt), ALU.mult).then_inc(S["step"], 1)
                    nc.vector.memset(state[:, 1, :], 0.0).then_inc(S["state0"], 1)
                    dve.wait_ge(S["exp"], 3)
                    dve.wait_ge(S["step"], 4)
                    nc.vector.tensor_tensor(heads(xw), heads(xdt), wide(wend), ALU.mult).then_inc(S["step"], 1)

                @block.scalar
                def _(act):
                    act.wait_ge(S["step"], 3)
                    nc.scalar.activation(ecum[:, :, :], cum[:, :, :], ACT.Exp).then_inc(S["exp"], 1)
                    nc.scalar.activation(wend[:, :, :], wend[:, :, :], ACT.Exp).then_inc(S["exp"], 1)
                    nc.scalar.activation(etot[:, :, :], etot[:, :, :], ACT.Exp).then_inc(S["exp"], 1)

        with net.phase("m_scan", ["skip", "skipped", "gated", "sq", "rows", "diff", "decay", "gmm", "mt", "intra", "inter", "smm", "scaled", "state", "part", "y"]) as (S, blk):
            ex = net.tmp("ex", [P, 2, H, P])
            mt = net.tmp("mt", [P, 2, H, P])
            part = net.tmp("part", [P, 2, DI])
            sdec = net.tmp("sdec", [N, DI])
            junk = net.tmp("junk", [P, 2, DI])
            pr = net.psum("pr", [P, 2, H, P])
            pg = net.psum("pg", [P, 2, HALF])
            py = net.psum("py", [P, 2, HALF])
            pn = net.psum("pn", [P, 2, HALF])
            with blk as block:
                @block.sync
                def _(sp):
                    net.clear_previous(sp)

                @block.gpsimd
                def _(pool):
                    for t in range(NT):
                        nc.gpsimd.tensor_tensor(x_tok[:, t, :].rearrange("p (h d) -> p h d", h=H), x_tok[:, t, :].rearrange("p (h d) -> p h d", h=H),
                                                W("l3_dv").unsqueeze(2).broadcast_to([P, H, D]), ALU.mult).then_inc(S["skip"], 1)
                        pool.wait_ge(S["skip"], t + 1)
                        pool.wait_ge(S["y"], t + 1)
                        nc.gpsimd.tensor_tensor(y_tok[:, t, :], y_tok[:, t, :], x_tok[:, t, :], ALU.add).then_inc(S["skipped"], 1)
                        pool.wait_ge(S["skipped"], t + 1)
                        nc.gpsimd.tensor_tensor(y_tok[:, t, :], y_tok[:, t, :], z_tok[:, t, :], ALU.mult).then_inc(S["gated"], 1)
                    pool.wait_ge(S["gated"], NT)

                @block.tensor
                def _(pe):
                    def decay_rows(t):
                        if t >= 2:
                            pe.wait_ge(S["diff"], t - 1)
                        for h in range(H):
                            nc.tensor.matmul(pr[:, t % 2, h, :], da[:, t, h:h + 1].broadcast_to([P, P]), net.K("tri"), start=True, stop=False)
                            last = nc.tensor.matmul(pr[:, t % 2, h, :], net.ident_bf, net.later_kq, start=False, stop=True)
                        last.then_inc(S["rows"], 1)
                        if t >= 2:
                            pe.wait_ge(S["mt"], t - 1)
                        ts = slice(t * P, (t + 1) * P)
                        nc.tensor.matmul(pg[:, t % 2, 0:P], b_ch[:, ts], c_ch[:, ts], start=True, stop=True).then_inc(S["gmm"], 1)

                    decay_rows(0)
                    for t in range(NT):
                        if t + 1 < NT:
                            decay_rows(t + 1)
                        ts = slice(t * P, (t + 1) * P)
                        if t >= 2:
                            pe.wait_ge(S["state"], t - 1)
                        nc.tensor.matmul(pn[0:N, t % 2, 0:DI], b_tok[:, t, :], xw[:, t, :], start=True, stop=True).then_inc(S["smm"], 1)
                        pe.wait_ge(S["mt"], t + 1)
                        if t >= 2:
                            pe.wait_ge(S["y"], t - 1)
                        for h in range(H):
                            last = nc.tensor.matmul(py[:, t % 2, h * D:(h + 1) * D], mt[:, t % 2, h, :], xdt[:, t, h * D:(h + 1) * D],
                                                    start=True, stop=True)
                        if t >= 1:
                            pe.wait_ge(S["state"], t)
                        nc.tensor.matmul(py[:, t % 2, DI:2 * DI], c_ch[:, ts], state[:, (t + 1) % 2, :], start=True, stop=True).then_inc(S["inter"], 1)

                @block.scalar
                def _(act):
                    def squares(t):
                        act.wait_ge(S["gated"], t + 1)
                        if t >= 2:
                            act.wait_ge(S["sq"], t - 1)
                        nc.scalar.activation(junk[:, t % 2, :], y_tok[:, t, :], ACT.Square, accum_out=ss[:, t:t + 1]).then_inc(S["sq"], 1)

                    for t in range(NT):
                        act.wait_ge(S["diff"], t + 1)
                        nc.scalar.activation(ex[:, t % 2, :, :], ex[:, t % 2, :, :], ACT.Exp).then_inc(S["decay"], 1)
                        if t >= 3:
                            squares(t - 3)
                    for t in range(NT - 3, NT):
                        squares(t)

                @block.vector
                def _(dve):
                    hd = lambda a: a.rearrange("p (h d) -> p h d", h=H)

                    def differences(t):
                        dve.wait_ge(S["rows"], t + 1)
                        if t >= 2:
                            dve.wait_ge(S["mt"], t - 1)
                        nc.vector.tensor_tensor(ex[:, t % 2, :, :], pr[:, t % 2, :, :], cum[:, t, :].unsqueeze(2).broadcast_to([P, H, P]),
                                                ALU.subtract).then_inc(S["diff"], 1)

                    def output(t):
                        dve.wait_ge(S["inter"], t + 1)
                        nc.vector.tensor_tensor(hd(part[:, t % 2, :]), hd(py[:, t % 2, DI:2 * DI]), ecum[:, t, :].unsqueeze(2).broadcast_to([P, H, D]),
                                                ALU.mult).then_inc(S["part"], 1)
                        dve.wait_ge(S["part"], t + 1)
                        nc.vector.tensor_tensor(y_tok[:, t, :], py[:, t % 2, 0:DI], part[:, t % 2, :], ALU.add).then_inc(S["y"], 1)

                    differences(0)
                    for t in range(NT):
                        dve.wait_ge(S["decay"], t + 1)
                        dve.wait_ge(S["gmm"], t + 1)
                        if t >= 2:
                            dve.wait_ge(S["inter"], t - 1)
                        nc.vector.tensor_tensor(mt[:, t % 2, :, :], pg[:, t % 2, 0:P].unsqueeze(1).broadcast_to([P, H, P]), ex[:, t % 2, :, :],
                                                ALU.mult).then_inc(S["mt"], 1)
                        if t + 1 < NT:
                            differences(t + 1)
                        if t >= 1:
                            dve.wait_ge(S["state"], t)
                        nc.vector.tensor_tensor(hd(sdec[:, :]), hd(state[:, (t + 1) % 2, :]), etot[0:N, t, :].unsqueeze(2).broadcast_to([N, H, D]),
                                                ALU.mult).then_inc(S["scaled"], 1)
                        dve.wait_ge(S["scaled"], t + 1)
                        dve.wait_ge(S["smm"], t + 1)
                        if t >= 1:
                            dve.wait_ge(S["inter"], t)
                        nc.vector.tensor_tensor(state[:, t % 2, :], pn[0:N, t % 2, 0:DI], sdec[:, :], ALU.add).then_inc(S["state"], 1)
                        if t >= 1:
                            output(t - 1)
                    output(NT - 1)

        with net.phase("m_out", ["step", "std", "normed", "turned", "ch", "mm", "done"]) as (S, blk):
            rs = net.tmp("rs", [P, NT])
            ych = net.tmp("ych", [P, 2, T])
            pt = net.psum("pt", [P, 4, HALF])
            po = net.psum("po", [P, 2, HALF])
            with blk as block:
                @block.sync
                def _(sp):
                    net.clear_previous(sp)

                @block.vector
                def _(dve):
                    n = [0]

                    def step(ins):
                        n[0] += 1
                        ins.then_inc(S["step"], 1)
                        dve.wait_ge(S["step"], n[0])

                    step(nc.vector.tensor_scalar(ss[:, :], ss[:, :], 1.0 / DI, EPS, ALU.mult, ALU.add))
                    dve.wait_ge(S["std"], 1)
                    step(nc.vector.reciprocal(rs[:, :], ss[:, :]))
                    for t in range(NT):
                        nc.vector.scalar_tensor_tensor(out=y_tok[:, t, :], in0=y_tok[:, t, :], scalar=rs[:, t:t + 1], in1=W("l3_rms"),
                                                       op0=ALU.mult, op1=ALU.mult).then_inc(S["normed"], 1)
                    for i in range(2):
                        dve.wait_ge(S["mm"], i + 1)
                        nc.vector.tensor_tensor(net.s_tok[:, 4 * i:4 * i + 4, :], po[:, i, :].rearrange("p (t c) -> p t c", t=4),
                                                net.xn_tok[:, 4 * i:4 * i + 4, :], ALU.add).then_inc(S["done"], 1)

                @block.scalar
                def _(act):
                    act.wait_ge(S["step"], 1)
                    nc.scalar.activation(ss[:, :], ss[:, :], ACT.Sqrt).then_inc(S["std"], 1)
                    for k in range(4):
                        act.wait_ge(S["turned"], k + 1)
                        nc.scalar.activation(ych[:, k % 2, k // 2 * HALF:(k // 2 + 1) * HALF], pt[:, k, :], ACT.Copy).then_inc(S["ch"], 1)

                @block.tensor
                def _(pe):
                    for i in range(2):
                        for j in range(2):
                            pe.wait_ge(S["normed"], 4 * (i + 1))
                            for q in range(4):
                                last = nc.tensor.transpose(pt[:, 2 * i + j, q * P:(q + 1) * P], y_tok[:, 4 * i + q, j * P:(j + 1) * P], net.ident)
                            last.then_inc(S["turned"], 1)
                    for i in range(2):
                        pe.wait_ge(S["ch"], 2 * (i + 1))
                        for t in range(4 * i, 4 * i + 4):
                            for j in range(2):
                                last = nc.tensor.matmul(po[:, i, t % 4 * C:(t % 4 + 1) * C], ych[:, j, t * P:(t + 1) * P], W("l3_out", 2, j),
                                                        start=(j == 0), stop=(j == 1))
                        last.then_inc(S["mm"], 1)


def shift_tokens(net, src, dst):
    nc = net.nc
    HC = C // 2
    with net.phase("shift", ["mm", "low", "high"]) as (S, blk):
        ps = net.psum("ps", [P, NT, HC])
        with blk as block:
            @block.sync
            def _(sp):
                net.clear_previous(sp)

            @block.tensor
            def _(pe):
                for t in range(NT):
                    last = nc.tensor.matmul(ps[:, t, :], net.K("shift"), src[:, t, HC:C], start=True, stop=(t == 0))
                    if t > 0:
                        last = nc.tensor.matmul(ps[:, t, :], net.K("carry"), src[:, t - 1, HC:C], start=False, stop=True)
                last.then_inc(S["mm"], 1)

            @block.scalar
            def _(act):
                nc.scalar.activation(dst[:, :, 0:HC], src[:, :, 0:HC], ACT.Copy).then_inc(S["low"], 1)

            @block.vector
            def _(dve):
                dve.wait_ge(S["mm"], 1)
                nc.vector.tensor_copy(dst[:, :, HC:C], ps[:, :, :]).then_inc(S["high"], 1)


def local_block(net, d):
    nc, W = net.nc, net.W
    H, D = 8, 64
    IN = H * D
    WINDOW = 64
    HID = 341
    hb = [(0, 128), (128, 128), (256, 85)]
    with ExitStack() as keep:
        def kept(name, shape):
            return keep.enter_context(nc.sbuf_tensor(f"{name}{d}", shape, F32))
        v_l = kept("lv", [P, NT, IN])
        qt = kept("lqt", [P, H // 2, T])
        kt = kept("lkt", [P, H // 2, T])
        shift_tokens(net, net.xn_tok, net.ctx_tok)
        with net.phase("l_qkv", ["turned", "ch", "scales", "qkmm", "vmm", "sq", "v", "sum", "std", "inv", "step", "unit", "kstep", "q", "k", "tq", "out"]) as (S, blk):
            tc = net.tmp("tc", [P, 2, NT, D])
            tsn = net.tmp("tsn", [P, 2, NT, D])
            sq = net.tmp("sq", [P, 2, IN])
            ss = net.tmp("ss", [P, 2, 2 * H])
            aq = net.tmp("aq", [P, IN])
            ak = net.tmp("ak", [P, 2, IN])
            rq = net.tmp("rq", [P, IN])
            rk = net.tmp("rk", [P, IN])
            qr = net.tmp("qr", [P, 2, IN])
            kr = net.tmp("kr", [P, 2, IN])
            pq = net.psum("pq", [P, 2, 2, IN])
            pv = net.psum("pv", [P, 2, IN])
            pt = net.psum("pt", [P, 2, IN])
            ch = net.xn_ch

            def copy_out(act, t):
                for m, dst in enumerate((qt, kt)):
                    act.wait_ge(S["tq"], 2 * t + m + 1)
                    nc.scalar.activation(dst[:, :, t * P:(t + 1) * P], pt[:, m, :].rearrange("p (j c) -> p j c", j=H // 2), ACT.Copy).then_inc(S["out"], 1)

            def rotate(ops, eng, stepped, ready, t, m, a, r, out):
                v3 = lambda x: x.rearrange("p (h d) -> p h d", h=H)
                half = D // 2
                b = lambda tab, lo, n: tab[:, m, t, lo:lo + n].unsqueeze(1).broadcast_to([P, H, n])
                ops.tensor_tensor(v3(out), v3(a), b(tc, 0, D), ALU.mult).then_inc(S[stepped], 1)
                if t >= 1:
                    eng.wait_ge(S[ready], t)
                for lo, other in ((0, half), (half, 0)):
                    ops.tensor_tensor(v3(r[:, :])[:, :, lo:lo + half], v3(a)[:, :, other:other + half], b(tsn, lo, half), ALU.mult).then_inc(S[stepped], 1)
                eng.wait_ge(S[stepped], 3 * t + 3)
                ops.tensor_tensor(out, out, r[:, :], ALU.add).then_inc(S[ready], 1)

            with blk as block:
                @block.sync
                def _(sp):
                    net.clear_previous(sp)

                @block.gpsimd
                def _(pool):
                    for m, (cn, sn, sc) in enumerate((("xq_cos", "xq_sin", f"l3_qs{d}"), ("xk_cos", "xk_sin", f"l3_ks{d}"))):
                        tab = lambda n: net.K(n).rearrange("p (t c) -> p t c", t=NT)
                        s = W(sc).unsqueeze(1)
                        nc.gpsimd.tensor_tensor(tc[:, m, :, :], tab(cn), s.broadcast_to([P, NT, D]), ALU.mult).then_inc(S["scales"], 1)
                        for lo, other in ((0, D // 2), (D // 2, 0)):
                            nc.gpsimd.tensor_tensor(tsn[:, m, :, lo:lo + D // 2], tab(sn)[:, :, lo:lo + D // 2],
                                                    s[:, :, other:other + D // 2].broadcast_to([P, NT, D // 2]), ALU.mult).then_inc(S["scales"], 1)
                    pool.wait_ge(S["scales"], 6)
                    for t in range(NT):
                        pool.wait_ge(S["unit"], 2 * t + 2)
                        if t >= 2:
                            pool.wait_ge(S["tq"], 2 * (t - 1))
                        rotate(nc.gpsimd, pool, "kstep", "k", t, 1, ak[:, t % 2, :], rk, kr[:, t % 2, :])

                @block.tensor
                def _(pe):
                    def qkv(t):
                        x = ch[:, t * P:(t + 1) * P]
                        if t >= 2:
                            pe.wait_ge(S["unit"], 2 * (t - 1))
                            pe.wait_ge(S["sq"], 2 * (t - 1))
                            pe.wait_ge(S["v"], t - 1)
                        for m in range(2):
                            last = nc.tensor.matmul(pq[:, t % 2, m, :], x, W(f"l3_wqkv{d}")[:, m * IN:(m + 1) * IN], start=True, stop=True)
                        last.then_inc(S["qkmm"], 1)
                        nc.tensor.matmul(pv[:, t % 2, :], x, W(f"l3_wqkv{d}")[:, 2 * IN:3 * IN], start=True, stop=True).then_inc(S["vmm"], 1)

                    for i in range(2):
                        for j in range(4):
                            last = nc.tensor.transpose(pt[:, i, j * P:(j + 1) * P], net.ctx_tok[:, 4 * i + j, :], net.ident)
                        last.then_inc(S["turned"], 1)
                    pe.wait_ge(S["ch"], 2)
                    qkv(0)
                    qkv(1)
                    for t in range(NT):
                        if t + 2 < NT:
                            qkv(t + 2)
                        for m, (src, name) in enumerate(((qr, "q"), (kr, "k"))):
                            pe.wait_ge(S[name], t + 1)
                            if t >= 1:
                                pe.wait_ge(S["out"], 2 * (t - 1) + m + 1)
                            for j in range(H // 2):
                                last = nc.tensor.transpose(pt[:, m, j * P:(j + 1) * P], src[:, t % 2, j * P:(j + 1) * P], net.ident)
                            last.then_inc(S["tq"], 1)

                @block.scalar
                def _(act):
                    for i in range(2):
                        act.wait_ge(S["turned"], i + 1)
                        nc.scalar.activation(ch[:, i * HALF:(i + 1) * HALF], pt[:, i, :], ACT.Copy).then_inc(S["ch"], 1)

                    def squares(t):
                        act.wait_ge(S["qkmm"], t + 1)
                        if t >= 1:
                            act.wait_ge(S["sum"], t)
                        for m in range(2):
                            nc.scalar.activation(sq[:, m, :], pq[:, t % 2, m, :], ACT.Square).then_inc(S["sq"], 1)
                        act.wait_ge(S["vmm"], t + 1)
                        nc.scalar.activation(v_l[:, t, :], pv[:, t % 2, :], ACT.Copy).then_inc(S["v"], 1)

                    squares(0)
                    for t in range(NT):
                        act.wait_ge(S["sum"], t + 1)
                        nc.scalar.activation(ss[:, t % 2, :], ss[:, t % 2, :], ACT.Sqrt).then_inc(S["std"], 1)
                        if t + 1 < NT:
                            squares(t + 1)
                        if t >= 1:
                            copy_out(act, t - 1)
                    copy_out(act, NT - 1)

                @block.vector
                def _(dve):
                    dve.wait_ge(S["scales"], 6)
                    def sums(t):
                        dve.wait_ge(S["sq"], 2 * t + 2)
                        if t >= 2:
                            dve.wait_ge(S["unit"], 2 * (t - 1))
                        nc.vector.tensor_reduce(ss[:, t % 2, :], sq[:, :, :].rearrange("p m (h d) -> p (m h) d", h=H), AX.X, ALU.add).then_inc(S["sum"], 1)

                    sums(0)
                    for t in range(NT):
                        dve.wait_ge(S["std"], t + 1)
                        nc.vector.tensor_scalar(ss[:, t % 2, :], ss[:, t % 2, :], 1e-12, None, ALU.max).then_inc(S["inv"], 1)
                        dve.wait_ge(S["inv"], 2 * t + 1)
                        nc.vector.reciprocal(ss[:, t % 2, :], ss[:, t % 2, :]).then_inc(S["inv"], 1)
                        dve.wait_ge(S["inv"], 2 * t + 2)
                        if t >= 1:
                            dve.wait_ge(S["step"], 3 * t)
                        if t >= 2:
                            dve.wait_ge(S["kstep"], 3 * (t - 1))
                        for m, dst in enumerate((aq[:, :], ak[:, t % 2, :])):
                            nc.vector.tensor_tensor(dst.rearrange("p (h d) -> p h d", h=H), pq[:, t % 2, m, :].rearrange("p (h d) -> p h d", h=H),
                                                    ss[:, t % 2, m * H:(m + 1) * H].unsqueeze(2).broadcast_to([P, H, D]), ALU.mult).then_inc(S["unit"], 1)
                        if t + 1 < NT:
                            sums(t + 1)
                        dve.wait_ge(S["unit"], 2 * t + 2)
                        if t >= 2:
                            dve.wait_ge(S["tq"], 2 * (t - 1))
                        rotate(nc.vector, dve, "step", "q", t, 0, aq[:, :], rq, qr[:, t % 2, :])

        with net.phase("l_att", ["zero", "s", "max", "exp", "exped", "tp", "copied", "o", "inv", "norm"]) as (S, blk):
            o_tok = kept("lo", [P, NT, IN])
            nm = net.tmp("nm", [P, 2, 4])
            pr = net.tmp("pr", [P, 2, 4, 2 * P])
            den = net.tmp("den", [P, 2, H])
            inv = net.tmp("inv", [P, H])
            ptr = net.tmp("ptr", [P, 2, 2, 2 * P])
            ps = net.psum("ps", [P, 2, 4, 2 * P])
            pt = net.psum("pt", [P, 2, 2, 2 * P])
            po = net.psum("po", [P, 2, IN])
            units = [(t, g) for t in range(NT) for g in range(2)]
            at = lambda i: i // 2 + 2 * (i % 2)
            lows = lambda t: P if t == 0 else P - WINDOW

            def normalise(dve, t):
                if t >= 1:
                    dve.wait_ge(S["norm"], t)
                dve.wait_ge(S["exped"], H * (t + 1))
                nc.vector.reciprocal(inv[:, :], den[:, t % 2, :]).then_inc(S["inv"], 1)
                dve.wait_ge(S["inv"], t + 1)
                dve.wait_ge(S["o"], 4 * (t + 1))
                nc.vector.tensor_tensor(o_tok[:, t, :].rearrange("p (h d) -> p h d", h=H), po[:, t % 2, :].rearrange("p (h d) -> p h d", h=H),
                                        inv[:, :].unsqueeze(2).broadcast_to([P, H, D]), ALU.mult).then_inc(S["norm"], 1)

            with blk as block:
                @block.sync
                def _(sp):
                    net.clear_previous(sp)

                @block.tensor
                def _(pe):
                    def scores(u):
                        t, g = units[u]
                        lo = lows(t)
                        if u >= 2:
                            pe.wait_ge(S["exped"], 4 * (u - 1))
                        k0 = (t - 1) * P + lo
                        for bank in range(2):
                            nc.tensor.matmul(ps[:, u % 2, 2 * bank:2 * bank + 2, lo:2 * P], net.ident_bf,
                                             net.local_qk[:, lo:2 * P].unsqueeze(1).broadcast_to([P, 2, 2 * P - lo]), start=True, stop=False)
                        for i in range(4):
                            h = 4 * g + i
                            b0 = D * (h % 2)
                            last = nc.tensor.matmul(ps[:, u % 2, at(i), lo:2 * P], qt[b0:b0 + D, h // 2, t * P:(t + 1) * P],
                                                    kt[b0:b0 + D, h // 2, k0:(t + 1) * P], start=False, stop=(i >= 2))
                        last.then_inc(S["s"], 1)

                    def turn(w):
                        u, half = divmod(w, 2)
                        t, g = units[u]
                        pe.wait_ge(S["exped"], 4 * (u + 1))
                        if w >= 2:
                            pe.wait_ge(S["copied"], w - 1)
                        for c in range(2):
                            for s in range(1 if t == 0 else 0, 2):
                                last = nc.tensor.transpose(pt[:, w % 2, c, s * P:(s + 1) * P], pr[:, u % 2, 2 * half + c, s * P:(s + 1) * P], net.ident)
                        last.then_inc(S["tp"], 1)

                    def weigh(w):
                        u, half = divmod(w, 2)
                        t, g = units[u]
                        pe.wait_ge(S["copied"], w + 1)
                        if w % 4 == 0 and t >= 2:
                            pe.wait_ge(S["norm"], t - 1)
                        first = 1 if t == 0 else 0
                        for c in range(2):
                            h = 4 * g + 2 * c + half
                            for s in range(first, 2):
                                last = nc.tensor.matmul(po[:, t % 2, h * D:(h + 1) * D], ptr[:, w % 2, c, s * P:(s + 1) * P],
                                                        v_l[:, t - 1 + s, h * D:(h + 1) * D], start=(s == first), stop=(s == 1))
                        last.then_inc(S["o"], 1)

                    scores(0)
                    scores(1)
                    pe.wait_ge(S["zero"], 1)
                    for u in range(len(units)):
                        turn(2 * u)
                        turn(2 * u + 1)
                        if u + 2 < len(units):
                            scores(u + 2)
                        weigh(2 * u)
                        weigh(2 * u + 1)

                @block.scalar
                def _(act):
                    for u, (t, g) in enumerate(units):
                        lo = lows(t)
                        act.wait_ge(S["max"], u + 1)
                        if u >= 2:
                            act.wait_ge(S["tp"], 2 * (u - 1))
                        if g == 0 and t >= 2:
                            act.wait_ge(S["inv"], t - 1)
                        for i in range(4):
                            c = at(i)
                            nc.scalar.activation(pr[:, u % 2, c, lo:2 * P], ps[:, u % 2, c, lo:2 * P], ACT.Exp, bias=nm[:, u % 2, c:c + 1],
                                                 accum_out=den[:, t % 2, 4 * g + i:4 * g + i + 1]).then_inc(S["exped"], 1)

                @block.vector
                def _(dve):
                    def maxima(u):
                        t, g = units[u]
                        dve.wait_ge(S["s"], u + 1)
                        if u >= 2:
                            dve.wait_ge(S["exped"], 4 * (u - 1))
                        nc.vector.tensor_reduce(nm[:, u % 2, :], ps[:, u % 2, :, lows(t):2 * P], AX.X, ALU.max, negate=True).then_inc(S["max"], 1)

                    nc.vector.memset(pr[:, :, :, 0:P - WINDOW].rearrange("p b h c -> p (b h) c"), 0.0).then_inc(S["zero"], 1)
                    maxima(0)
                    for u, (t, g) in enumerate(units):
                        if u + 1 < len(units):
                            maxima(u + 1)
                        for w in (2 * u, 2 * u + 1):
                            dve.wait_ge(S["tp"], w + 1)
                            if w >= 2:
                                dve.wait_ge(S["o"], w - 1)
                            lo = P if t == 0 else 0
                            nc.vector.tensor_copy(ptr[:, w % 2, :, lo:2 * P], pt[:, w % 2, :, lo:2 * P]).then_inc(S["copied"], 1)
                        if g == 0 and t >= 1:
                            normalise(dve, t - 1)
                    normalise(dve, NT - 1)

        with net.phase("l_wo", ["turned", "ch", "mm", "sum"]) as (S, blk):
            och = net.tmp("och", [P, 2, IN])
            pt = net.psum("pt", [P, 2, IN])
            po = net.psum("po", [P, 2, HALF])
            with blk as block:
                @block.sync
                def _(sp):
                    net.clear_previous(sp)

                @block.tensor
                def _(pe):
                    def turn(t):
                        if t >= 2:
                            pe.wait_ge(S["ch"], t - 1)
                        for j in range(4):
                            last = nc.tensor.transpose(pt[:, t % 2, j * P:(j + 1) * P], o_tok[:, t, j * P:(j + 1) * P], net.ident)
                        last.then_inc(S["turned"], 1)

                    turn(0)
                    for t in range(NT):
                        if t + 1 < NT:
                            turn(t + 1)
                        pe.wait_ge(S["ch"], t + 1)
                        if t >= 2:
                            pe.wait_ge(S["sum"], t - 1)
                        for j in range(4):
                            last = nc.tensor.matmul(po[:, t % 2, 0:C], och[:, t % 2, j * P:(j + 1) * P], W(f"l3_wo{d}", 4, j),
                                                    start=(j == 0), stop=(j == 3))
                        last.then_inc(S["mm"], 1)

                @block.scalar
                def _(act):
                    for t in range(NT):
                        act.wait_ge(S["turned"], t + 1)
                        if t >= 2:
                            act.wait_ge(S["mm"], t - 1)
                        nc.scalar.activation(och[:, t % 2, :], pt[:, t % 2, :], ACT.Copy).then_inc(S["ch"], 1)

                @block.vector
                def _(dve):
                    for t in range(NT):
                        dve.wait_ge(S["mm"], t + 1)
                        nc.vector.tensor_tensor(net.xn_tok[:, t, :], po[:, t % 2, 0:C], net.xn_tok[:, t, :], ALU.add).then_inc(S["sum"], 1)

    shift_tokens(net, net.xn_tok, net.ctx_tok)
    layer_norm(net, net.ctx_tok, None, net.in_ch, gamma=W(f"l3_lg{d}"), beta=W(f"l3_lb{d}"))
    units = [(c, j) for c in range(2) for j in range(3)]
    with net.phase("l_ffn", ["mm", "gelu", "hid", "outp", "biased", "sum"]) as (S, blk):
        gg = net.tmp("gg", [P, 2, HALF])
        h = net.tmp("h", [P, 3, T])
        pa = net.psum("pa", [P, 2, HALF])
        pg = net.psum("pg", [P, 2, HALF])
        po = net.psum("po", [P, 2, HALF])
        with blk as block:
            @block.sync
            def _(sp):
                net.clear_previous(sp)

            @block.tensor
            def _(pe):
                for u, (c, j) in enumerate(units):
                    c0, m = hb[j]
                    x = net.in_ch[:, c * HALF:(c + 1) * HALF]
                    if u >= 2:
                        pe.wait_ge(S["hid"], u - 1)
                    nc.tensor.matmul(pg[0:m, u % 2, :], W(f"l3_w1{d}")[:, HID + c0:HID + c0 + m], x, start=True, stop=True)
                    nc.tensor.matmul(pa[0:m, u % 2, :], W(f"l3_w1{d}")[:, c0:c0 + m], x, start=True, stop=True).then_inc(S["mm"], 1)
                for c in range(2):
                    pe.wait_ge(S["hid"], 3 * (c + 1))
                    for t in range(4 * c, 4 * c + 4):
                        for j, (c0, m) in enumerate(hb):
                            last = nc.tensor.matmul(po[:, c, t % 4 * C:(t % 4 + 1) * C], h[0:m, j, t * P:(t + 1) * P], W(f"l3_w2{d}", 3, j)[0:m, :],
                                                    start=(j == 0), stop=(j == 2))
                    last.then_inc(S["outp"], 1)

            @block.scalar
            def _(act):
                for u, (c, j) in enumerate(units):
                    c0, m = hb[j]
                    act.wait_ge(S["mm"], u + 1)
                    if u >= 2:
                        act.wait_ge(S["hid"], u - 1)
                    nc.scalar.activation(gg[0:m, u % 2, :], pg[0:m, u % 2, :], ACT.Gelu, bias=W(f"l3_b1g{d}", 3, j)[0:m, :]).then_inc(S["gelu"], 1)

            @block.vector
            def _(dve):
                nc.vector.tensor_tensor(net.xn_tok[:, :, :], net.xn_tok[:, :, :], W(f"l3_b2{d}").unsqueeze(1).broadcast_to([P, NT, C]),
                                        ALU.add).then_inc(S["biased"], 1)
                for u, (c, j) in enumerate(units):
                    c0, m = hb[j]
                    dve.wait_ge(S["gelu"], u + 1)
                    dve.wait_ge(S["mm"], u + 1)
                    nc.vector.scalar_tensor_tensor(out=h[0:m, j, c * HALF:(c + 1) * HALF], in0=pa[0:m, u % 2, :], scalar=W(f"l3_b1a{d}", 3, j)[0:m, :],
                                                   in1=gg[0:m, u % 2, :], op0=ALU.add, op1=ALU.mult).then_inc(S["hid"], 1)
                dve.wait_ge(S["biased"], 1)
                for c in range(2):
                    dve.wait_ge(S["outp"], c + 1)
                    nc.vector.tensor_tensor(net.xn_tok[:, 4 * c:4 * c + 4, :], po[:, c, :].rearrange("p (t c) -> p t c", t=4),
                                            net.xn_tok[:, 4 * c:4 * c + 4, :], ALU.add).then_inc(S["sum"], 1)


LAYERS = 4


def build(nc, x, out, packs, wheres, consts, const_where, streams, stream_where):
    ctx = ExitStack()
    with ctx:
        net = Net(nc, ctx)
        resident = [net.sbuf(f"w{i}", [P, p.shape[1]]) for i, p in enumerate(packs)]
        table = net.sbuf("table", [P, consts.shape[1]])

        def W(name, blocks=1, j=0):
            for buf, where in zip(resident, wheres):
                if name in where:
                    o, n, r = where[name]
                    n //= blocks
                    return buf[0:r, o + j * n:o + (j + 1) * n]
            raise KeyError(name)

        def K(name):
            o, n, r = const_where[name]
            return table[0:r, o:o + n]

        net.W, net.K = W, K
        net.streams, net.stream_where = streams, stream_where
        net.loads = [(table[:, :], consts)] + [(b[:, :], p) for b, p in zip(resident, packs)]
        net.ident, net.rope_cos, net.rope_sin = K("ident"), K("rope_cos"), K("rope_sin")
        net.casts = []

        def exact_bf16(name):
            src = K(name)
            buf = net.sbuf(name + "_bf", [P, src.shape[1]], BF16)
            net.casts.append((buf[:, :], src))
            return buf[:, :]

        net.ident_bf = exact_bf16("ident")
        net.later_qk, net.later_kq = exact_bf16("later_qk"), exact_bf16("later_kq")
        net.band_qk, net.band_kq = exact_bf16("band_qk"), exact_bf16("band_kq")
        net.local_qk = exact_bf16("local_qk")
        net.zeros_bf = net.sbuf("zeros_bf", [P, HALF], BF16)
        net.x_tok = net.sbuf("x_tok", [P, NT, C])
        net.xn_tok = net.sbuf("xn_tok", [P, NT, C])
        net.s_tok = net.sbuf("s_tok", [P, NT, C])
        net.g_tok = net.sbuf("g_tok", [P, NT, C])
        net.ctx_tok = net.sbuf("ctx_tok", [P, NT, C])
        net.v_tok = net.sbuf("v_tok", [P, NT, C])
        net.top = net.sbuf("top", [P, NT, 8])
        net.top_i = net.sbuf("top_i", [P, NT, 8])
        net.count = net.sbuf("count", [P, 8])
        net.xn_ch = net.sbuf("xn_ch", [P, T])
        net.in_ch = net.sbuf("in_ch", [P, T])
        net.q_scr = nc.dram_tensor("q_scr", [NH, 3, DH, T], BF16, kind="Internal").ap()
        net.k_scr = nc.dram_tensor("k_scr", [NH, 5, DH, T], BF16, kind="Internal").ap()
        net.y_scr = nc.dram_tensor("y_scr", [T, C], F32, kind="Internal").ap()

        load_constants(net)
        root = DH ** -0.5
        with nc.Fori(0, B) as b:
            rows = x[b].rearrange("(t p) c -> p t c", p=P)
            layer_norm(net, net.x_tok, None, net.xn_ch, load=rows)
            with attention_inputs(net):
                project_qkv(net, net.xn_ch, {k: W("l0_w" + k) for k in ("q", "qs", "k", "ks", "v")}, rope=True)
                rwkv_ffn(net, net.g_tok)
                attention(net, "band", root)
            linear_tok(net, net.ctx_tok, W("l0_wo"), net.s_tok)
            gate_update(net, net.g_tok)
            if LAYERS >= 2:
                layer_norm(net, net.x_tok, None, net.xn_ch)
                with attention_inputs(net):
                    project_qkv(net, net.xn_ch, {k: W("l1_w" + k) for k in ("q", "k", "v")},
                                bias={k: W("l1_b" + k) for k in "qkv"})
                    moe(net, net.g_tok)
                    attention(net, "causal", root)
                linear_tok(net, net.ctx_tok, W("l1_wo"), net.s_tok, bias=W("l1_bo"))
                gate_update(net, net.g_tok)
            if LAYERS >= 3:
                layer_norm(net, net.x_tok, net.xn_tok, net.xn_ch)
                layer_norm(net, net.xn_tok, None, net.in_ch, gamma=W("l2_g1"), beta=W("l2_be1"))
                with attention_inputs(net):
                    project_qkv(net, net.in_ch, {k: W("l2_w" + k) for k in ("q", "qs", "k", "ks", "v")},
                                bias={k: W("l2_b" + k) for k in "qkv"}, bias_s={k: W("l2_b" + k + "s") for k in "qk"}, rope=True)
                    switch_ffn(net, net.g_tok)
                    attention(net, "full", root)
                linear_tok(net, net.ctx_tok, W("l2_wo"), net.s_tok, bias=W("l2_bo"), plus=net.xn_tok)
                layer_norm(net, net.s_tok, None, net.in_ch, gamma=W("l2_g2"), beta=W("l2_be2"))
                relu_ffn(net)
                gate_update(net, net.g_tok)
            if LAYERS >= 4:
                layer_norm(net, net.x_tok, net.xn_tok, net.xn_ch)
                layer_norm(net, net.xn_tok, None, net.in_ch, gamma=W("l3_lnw"), beta=W("l3_lnb"))
                mamba(net)
                for d in range(2):
                    local_block(net, d)
                gate_update(net, net.xn_tok)
            store(net, out[b].rearrange("(t p) c -> p t c", p=P))


def store(net, dst):
    with net.phase("store", ["written"]) as (S, blk), blk as block:
        @block.sync
        def _(sp):
            net.clear_previous(sp)
            sp.dma_start(dst, net.x_tok[:, :, :]).then_inc(S["written"], 16)
            sp.wait_ge(S["written"], 16)
    with net.phase("end", []) as (S, blk), blk as block:
        @block.sync
        def _(sp):
            net.clear_previous(sp)
    net.end_of_row()


def kernel(**inputs):
    import concourse.bacc as bacc
    from concourse.bass_utils import run_bass_kernel_spmd

    nc = bacc.Bacc("TRN2", target_bir_lowering=False, num_devices=1)
    arrays = {}

    def feed(name, a):
        arrays[name] = np.ascontiguousarray(a)
        return nc.dram_tensor(name, arrays[name].shape, mybir.dt.from_np(arrays[name].dtype), kind="ExternalInput").ap()

    x = feed("x", inputs["L0_attn_query"])
    packs, wheres = [], []
    for n, group in enumerate(weights_of(inputs)):
        packed, where = pack_columns(group)
        packs.append(feed(f"weights_{n}", packed))
        wheres.append(where)
    packed, const_where = pack_columns(constants())
    consts = feed("tables", packed)
    packed, stream_where = pack_columns(switch_weights_of(inputs))
    streams = feed("switch_weights", packed)
    out = nc.dram_tensor("y", x.shape, F32, kind="ExternalOutput").ap()
    build(nc, x, out, packs, wheres, consts, const_where, streams, stream_where)
    r = run_bass_kernel_spmd(nc, [arrays], core_ids=[0])
    return r.results[0]["y"]
```
